# Optimizing a Trainium2 kernel written in Bass

```python
import numpy as np
import jax
import jax.numpy as jnp

def _softmax(x, axis=-1):
    return jax.nn.softmax(x, axis=axis)

def _gelu(x):
    return jax.nn.gelu(x, approximate=True)

def _silu(x):
    return jax.nn.silu(x)

def _sigmoid(x):
    return jax.nn.sigmoid(x)

def _layernorm(x, axis=-1, eps=1e-05):
    m = jnp.mean(x, axis=axis, keepdims=True)
    v = jnp.var(x, axis=axis, keepdims=True)
    return (x - m) / jnp.sqrt(v + eps)

def _scatter_add(tgt, idx, src, axis=0):
    return tgt.at[idx].add(src)

def _segment_sum(src, seg, n):
    return jax.ops.segment_sum(src, seg, n)
kernel_name = 'mk_gnn_resnorm_d1_gnn_r32_6c48cc'

def setup_inputs(seed: int=0):
    np.random.seed(seed)
    _w = jnp.asarray

    def _rec_inputs():
        import jax
        import jax.numpy as jnp
        _gk = jax.random.key(seed)
        x = -0.000202 + 1 * jax.random.normal(jax.random.fold_in(_gk, 1), (3125, 128), jnp.float32)
        src = jax.random.randint(jax.random.fold_in(_gk, 2), (100000,), 0, 3125, jnp.int32)
        dst = jnp.minimum((3125 * jax.random.uniform(jax.random.fold_in(_gk, 3), (100000,)) ** 2.0).astype(jnp.int32), 99999)
        _o = jnp.argsort(dst, stable=True)
        src = src[_o]
        dst = dst[_o]
        return (x, src, dst)
    x, src, dst = _rec_inputs()

    def _L0_gnn_setup():
        import jax, jax.numpy as jnp
        import numpy as np
        N, E, D, H, L, FF = (50000, 15625, 128, 8, 2, 512)
        HD = D // H

        def _layernorm(x, g, b):
            mu = jnp.mean(x, axis=-1, keepdims=True)
            var = jnp.mean(jnp.square(x - mu), axis=-1, keepdims=True)
            return (x - mu) * jax.lax.rsqrt(var + 1e-05) * g + b

        def _forward(edge_index, x, Wq, bq, Wk, bk, Wv, bv, Wo, bo, Wpos, bpos, Wdeg, bdeg, ln1_g, ln1_b, ln2_g, ln2_b, W1, b1, W2, b2):
            n = x.shape[0]
            loops = jnp.arange(n, dtype=edge_index.dtype)
            src = jnp.concatenate([edge_index[0], loops])
            dst = jnp.concatenate([edge_index[1], loops])
            scale = np.float32(np.sqrt(HD))
            for l in range(L):
                xn = _layernorm(x, ln1_g[l], ln1_b[l])
                deg = jax.ops.segment_sum(jnp.ones_like(src, dtype=x.dtype), src, num_segments=n)
                deg = (deg - deg.mean()) / (jnp.std(deg, ddof=1) + 1e-06)
                pos = xn @ Wpos[l] + bpos[l] + deg[:, None] * Wdeg[l][0] + bdeg[l]
                xp = xn + pos
                q = (xp @ Wq[l] + bq[l]).reshape(n, H, HD)
                k = (xp @ Wk[l] + bk[l]).reshape(n, H, HD)
                v = (xp @ Wv[l] + bv[l]).reshape(n, H, HD)
                att = jnp.einsum('ehd,ehd->eh', q[dst], k[src]) / scale
                att = jnp.nan_to_num(jnp.clip(att, -50.0, 50.0), nan=0.0, posinf=50.0, neginf=-50.0)
                m = jax.ops.segment_max(att, dst, num_segments=n)
                ex = jnp.exp(att - m[dst])
                s = jax.ops.segment_sum(ex, dst, num_segments=n)
                alpha = ex / (s[dst] + 1e-16)
                msg = (v[src] * alpha[:, :, None]).reshape(-1, D)
                aggr = jax.ops.segment_sum(msg, dst, num_segments=n)
                x = x + (aggr @ Wo[l] + bo[l])
                h = jax.nn.gelu(_layernorm(x, ln2_g[l], ln2_b[l]) @ W1[l] + b1[l], approximate=False)
                x = x + (h @ W2[l] + b2[l])
            return x
        key = jax.random.key(seed)
        ks = jax.random.split(key, 16)
        inp = {'x': jax.random.normal(ks[0], (N, D), jnp.float32), 'edge_index': jax.random.randint(ks[1], (2, E), 0, N, jnp.int32)}

        def w(k, shape, fan_in):
            return jax.random.normal(k, shape, jnp.float32) / np.float32(np.sqrt(fan_in))
        inp['Wq'] = w(ks[2], (L, D, D), D)
        inp['Wk'] = w(ks[3], (L, D, D), D)
        inp['Wv'] = w(ks[4], (L, D, D), D)
        inp['Wo'] = w(ks[5], (L, D, D), D)
        inp['Wpos'] = w(ks[6], (L, D, D), D)
        inp['Wdeg'] = w(ks[7], (L, 1, D), 1)
        inp['W1'] = w(ks[8], (L, D, FF), D)
        inp['W2'] = w(ks[9], (L, FF, D), FF)
        for name, shape in [('bq', (L, D)), ('bk', (L, D)), ('bv', (L, D)), ('bo', (L, D)), ('bpos', (L, D)), ('bdeg', (L, D)), ('ln1_b', (L, D)), ('ln2_b', (L, D)), ('b1', (L, FF)), ('b2', (L, D))]:
            inp[name] = jnp.zeros(shape, jnp.float32)
        inp['ln1_g'] = jnp.ones((L, D), jnp.float32)
        inp['ln2_g'] = jnp.ones((L, D), jnp.float32)
        return inp
    _L0_gnn_all = _L0_gnn_setup()
    _L0_gnn_in = {k: v for k, v in _L0_gnn_all.items() if k in ('Wq', 'bq', 'Wk', 'bk', 'Wv', 'bv', 'Wo', 'bo', 'Wpos', 'bpos', 'Wdeg', 'bdeg', 'ln1_g', 'ln1_b', 'ln2_g', 'ln2_b', 'W1', 'b1', 'W2', 'b2')}
    del _L0_gnn_all
    return {'x': x, 'src': src, 'dst': dst, 'L0_gnn_Wq': _L0_gnn_in['Wq'], 'L0_gnn_bq': _L0_gnn_in['bq'], 'L0_gnn_Wk': _L0_gnn_in['Wk'], 'L0_gnn_bk': _L0_gnn_in['bk'], 'L0_gnn_Wv': _L0_gnn_in['Wv'], 'L0_gnn_bv': _L0_gnn_in['bv'], 'L0_gnn_Wo': _L0_gnn_in['Wo'], 'L0_gnn_bo': _L0_gnn_in['bo'], 'L0_gnn_Wpos': _L0_gnn_in['Wpos'], 'L0_gnn_bpos': _L0_gnn_in['bpos'], 'L0_gnn_Wdeg': _L0_gnn_in['Wdeg'], 'L0_gnn_bdeg': _L0_gnn_in['bdeg'], 'L0_gnn_ln1_g': _L0_gnn_in['ln1_g'], 'L0_gnn_ln1_b': _L0_gnn_in['ln1_b'], 'L0_gnn_ln2_g': _L0_gnn_in['ln2_g'], 'L0_gnn_ln2_b': _L0_gnn_in['ln2_b'], 'L0_gnn_W1': _L0_gnn_in['W1'], 'L0_gnn_b1': _L0_gnn_in['b1'], 'L0_gnn_W2': _L0_gnn_in['W2'], 'L0_gnn_b2': _L0_gnn_in['b2']}

def reference(x, src, dst, L0_gnn_Wq, L0_gnn_bq, L0_gnn_Wk, L0_gnn_bk, L0_gnn_Wv, L0_gnn_bv, L0_gnn_Wo, L0_gnn_bo, L0_gnn_Wpos, L0_gnn_bpos, L0_gnn_Wdeg, L0_gnn_bdeg, L0_gnn_ln1_g, L0_gnn_ln1_b, L0_gnn_ln2_g, L0_gnn_ln2_b, L0_gnn_W1, L0_gnn_b1, L0_gnn_W2, L0_gnn_b2):
    import jax
    import jax.numpy as jnp

    def _L0_gnn_ref(x, edge_index, Wq, bq, Wk, bk, Wv, bv, Wo, bo, Wpos, bpos, Wdeg, bdeg, ln1_g, ln1_b, ln2_g, ln2_b, W1, b1, W2, b2):
        import jax, jax.numpy as jnp
        import numpy as np
        N, E, D, H, L, FF = (50000, 15625, 128, 8, 2, 512)
        HD = D // H

        def _layernorm(x, g, b):
            mu = jnp.mean(x, axis=-1, keepdims=True)
            var = jnp.mean(jnp.square(x - mu), axis=-1, keepdims=True)
            return (x - mu) * jax.lax.rsqrt(var + 1e-05) * g + b

        def _forward(edge_index, x, Wq, bq, Wk, bk, Wv, bv, Wo, bo, Wpos, bpos, Wdeg, bdeg, ln1_g, ln1_b, ln2_g, ln2_b, W1, b1, W2, b2):
            n = x.shape[0]
            loops = jnp.arange(n, dtype=edge_index.dtype)
            src = jnp.concatenate([edge_index[0], loops])
            dst = jnp.concatenate([edge_index[1], loops])
            scale = np.float32(np.sqrt(HD))
            for l in range(L):
                xn = _layernorm(x, ln1_g[l], ln1_b[l])
                deg = jax.ops.segment_sum(jnp.ones_like(src, dtype=x.dtype), src, num_segments=n)
                deg = (deg - deg.mean()) / (jnp.std(deg, ddof=1) + 1e-06)
                pos = xn @ Wpos[l] + bpos[l] + deg[:, None] * Wdeg[l][0] + bdeg[l]
                xp = xn + pos
                q = (xp @ Wq[l] + bq[l]).reshape(n, H, HD)
                k = (xp @ Wk[l] + bk[l]).reshape(n, H, HD)
                v = (xp @ Wv[l] + bv[l]).reshape(n, H, HD)
                att = jnp.einsum('ehd,ehd->eh', q[dst], k[src]) / scale
                att = jnp.nan_to_num(jnp.clip(att, -50.0, 50.0), nan=0.0, posinf=50.0, neginf=-50.0)
                m = jax.ops.segment_max(att, dst, num_segments=n)
                ex = jnp.exp(att - m[dst])
                s = jax.ops.segment_sum(ex, dst, num_segments=n)
                alpha = ex / (s[dst] + 1e-16)
                msg = (v[src] * alpha[:, :, None]).reshape(-1, D)
                aggr = jax.ops.segment_sum(msg, dst, num_segments=n)
                x = x + (aggr @ Wo[l] + bo[l])
                h = jax.nn.gelu(_layernorm(x, ln2_g[l], ln2_b[l]) @ W1[l] + b1[l], approximate=False)
                x = x + (h @ W2[l] + b2[l])
            return x
        return _forward(edge_index, x, Wq, bq, Wk, bk, Wv, bv, Wo, bo, Wpos, bpos, Wdeg, bdeg, ln1_g, ln1_b, ln2_g, ln2_b, W1, b1, W2, b2)
    edge_index = jnp.stack([src, dst])
    x = _layernorm(x + _L0_gnn_ref(x, edge_index, L0_gnn_Wq, L0_gnn_bq, L0_gnn_Wk, L0_gnn_bk, L0_gnn_Wv, L0_gnn_bv, L0_gnn_Wo, L0_gnn_bo, L0_gnn_Wpos, L0_gnn_bpos, L0_gnn_Wdeg, L0_gnn_bdeg, L0_gnn_ln1_g, L0_gnn_ln1_b, L0_gnn_ln2_g, L0_gnn_ln2_b, L0_gnn_W1, L0_gnn_b1, L0_gnn_W2, L0_gnn_b2), axis=-1)
    return x

_drawn_inputs = setup_inputs


def setup_inputs(seed=0):
    import zlib

    import numpy as np

    out = dict(_drawn_inputs(seed))
    spreads = {'L0_gnn_bq': (0.0, 0.1),
     'L0_gnn_bk': (0.0, 0.1),
     'L0_gnn_bv': (0.0, 0.1),
     'L0_gnn_bo': (0.0, 0.1),
     'L0_gnn_bpos': (0.0, 0.1),
     'L0_gnn_bdeg': (0.0, 0.1),
     'L0_gnn_ln1_g': (1.0, 0.2),
     'L0_gnn_ln1_b': (0.0, 0.1),
     'L0_gnn_ln2_g': (1.0, 0.2),
     'L0_gnn_ln2_b': (0.0, 0.1),
     'L0_gnn_b1': (0.0, 0.1),
     'L0_gnn_b2': (0.0, 0.1)}
    factors = {}
    for name, (base, spread) in spreads.items():
        noise = np.random.default_rng([zlib.crc32(name.encode()), seed]).standard_normal(out[name].shape)
        drawn = base * np.exp(spread * noise) if base else spread * noise
        out[name] = jnp.asarray(drawn.astype(out[name].dtype))
    for name, factor in factors.items():
        out[name] = (out[name] * factor).astype(out[name].dtype)
    return out
```

```python
import numpy as np
import concourse.bass as bass
from concourse import mybir
from contextlib import ExitStack

F32 = mybir.dt.float32
BF16 = mybir.dt.bfloat16
I32 = mybir.dt.int32
ALU = mybir.AluOpType
ACT = mybir.ActivationFunctionType
AX = mybir.AxisListType

N, E, D, H, L, FF = 3125, 100000, 128, 8, 2, 512
HD = D // H
P = 128
NT = -(-N // P)
NLAST = N - (NT - 1) * P
GC = 8
GE = GC * P
NG = -(-E // GE)
ELAST = E - (NG - 1) * GE
MW = D + H
SLOTS = 4
UN = 5
NU = NT // UN
FC = FF // P
LO = 64
HI = -(-N // LO)
HB = 28
NHB = NG * GC // HB
EPS = 1e-5
CLIP = 50.0
SCALE = float(HD) ** 0.5
MEAN_DEG = (E + N) / N
TOFF = 32
MAXPAIRS = NG * NT
assert NT % UN == 0 and NHB * HB == NG * GC and NHB % 2 == 0 and NG % SLOTS == 2


def gnn_program(nc, x_d, src_d, dst_d, W, out_d):
    ctx = ExitStack()
    with ctx:
        def sb(name, shape, dt=F32):
            return ctx.enter_context(nc.sbuf_tensor(name, shape, dt))

        def sem(name):
            return ctx.enter_context(nc.semaphore(name))

        def spread(ap, axis, n):
            new = ap.unsqueeze(axis)
            shape = list(new.shape)
            shape[axis] = n
            return new.broadcast_to(shape)

        def sems(name, n=L):
            return [sem(f"{name}{i}") for i in range(n)]

        x = sb("x", [P, NT, D])
        qkv = sb("qkv", [P, NT, 3 * D])
        q_parts = sb("q_parts", [P, NT, 3 * D], BF16)
        acc = sb("acc", [P, NT, MW])
        x_first = qkv[:, :, 0:D]
        kv = sb("kv", [P, SLOTS, GC, 2 * D])
        dst_hi = sb("dst_hi", [NG, GE], BF16)
        dst_lo = sb("dst_lo", [NG, GE], BF16)
        dst_col = sb("dst_col", [P, GC, NG])
        src_idx = sb("src_idx", [P, GC, NG], I32)
        idx = sb("idx", [P, SLOTS, GC], I32)
        pair_tab = sb("pair_tab", [1, 3, NG], I32)
        dist = sb("dist", [P, GE], BF16)
        hotT = sb("hotT", [P, 2, GE], BF16)
        hot = sb("hot", [P, GC, P])
        prod = sb("prod", [P, GE])
        dots = sb("dots", [P, GC * H])
        not_nan = sb("not_nan", [P, GC * H])
        clipped = sb("clipped", [P, GC * H])
        att = sb("att", [P, GC * H])
        msg = sb("msg", [P, GC, MW])
        ident = sb("ident", [P, P])
        ones = sb("ones", [P, P])
        zeros = sb("zeros", [P, 512], BF16)
        below = sb("below", [NG, NG])
        row_pick = sb("row_pick", [NG, NG, P], BF16)
        node_row = sb("node_row", [P, NT * P])
        neg_node = sb("neg_node", [P, NT])
        is_node = sb("is_node", [P, NT])
        eps_col = sb("eps_col", [P, 1])
        wqkv = sb("wqkv", [P, 3 * D])
        wpos = sb("wpos", [P, D])
        wfold = sb("wfold", [P, 3 * D])
        wo = sb("wo", [P, D])
        w1 = sb("w1", [P, FF])
        w1g = sb("w1g", [P, FF])
        w2 = sb("w2", [P, FC, D])
        vecs = sb("vecs", [P, 6])
        wdeg_col = sb("wdeg_col", [P, 1])
        b1_col = sb("b1_col", [P, FC])
        b1f = sb("b1f", [P, FC])
        bqkv_bc = sb("bqkv_bc", [P, 3 * D])
        bfold = sb("bfold", [P, 3 * D])
        degw = sb("degw", [P, 3 * D])
        bo_bc = sb("bo_bc", [P, D])
        b2_bc = sb("b2_bc", [P, D])
        cvec = sb("cvec", [P, 2])
        posT, pos1, c_bc, wd_bc = (hot[:, k, :] for k in range(4))
        stats = sb("stats", [P, NT, 6])
        half_gap = sb("half_gap", [P, NT])
        mean2 = sb("mean2", [P, NT])
        sq_dev = sb("sq_dev", [P, NT])
        gap2 = sb("gap2", [P, NT])
        var = sb("var", [P, NT])
        sd = sb("sd", [P, NT])
        rstd = sb("rstd", [P, NT])
        nmr = sb("nmr", [P, NT])
        dev = sb("dev", [P, NT])
        dev2 = sb("dev2", [P, NT])
        degn = sb("degn", [P, NT])
        dcol = sb("dcol", [P, 4])
        rsum = sb("rsum", [P, UN, H])
        z = sb("z", [P, UN, D])
        zT = sb("zT", [P, UN, D])
        kv_flat = kv[:, :, :, :].rearrange("p s c d -> p (s c d)")

        def row_buf(k, dt=F32):
            return kv_flat[0:NG, k * GE:(k + 1) * GE].bitcast(dt) if dt != F32 else kv_flat[0:NG, k * GE:(k + 1) * GE]

        src_i, dst_i, src_f, dst_f, tmp_f = row_buf(0, I32), row_buf(1, I32), row_buf(2), row_buf(3), row_buf(4)
        tmp_i = row_buf(5, I32)
        tmp_j = row_buf(6, I32)
        ext = sb("ext", [NG, 2])
        ext_i = sb("ext_i", [NG, 2], I32)
        ext_t = sb("ext_t", [NG, 2], I32)
        tiles = sb("tiles", [NG, 2])
        npair = sb("npair", [NG, 1])
        pair_f = prod[0:1, 0:3 * NG].rearrange("a (k g) -> a k g", g=NG)
        qf = q_parts[:, :, :].rearrange("p t d -> p (t d)")
        EC = NG * GC

        def carve(at, a, b):
            return qf[:, at:at + a * b].rearrange("p (a b) -> p a b", b=b)

        hot_lo = [carve(i * LO * HB, LO, HB) for i in range(2)]
        hot_hi = [carve(2 * LO * HB + i * HI * HB, HI, HB) for i in range(2)]
        AT = 2 * (LO + HI) * HB
        lo_ref = carve(AT, LO, HB)
        AT2 = AT + LO * HB
        qkv_flat = qkv[:, :, :].rearrange("p t d -> p (t d)")
        hi_ref = qkv_flat[:, 0:HI * HB // 2].bitcast(BF16).rearrange("p (a b) -> p a b", b=HB)
        src_lo = qkv_flat[:, 1000:1000 + EC // 2].bitcast(BF16)
        src_hi = qkv_flat[:, 1400:1400 + EC // 2].bitcast(BF16)
        src_ci = qkv_flat[:, 2000:2000 + EC].bitcast(I32)
        lo_i = qkv_flat[:, 3000:3000 + EC].bitcast(I32)
        hi_i = qkv_flat[:, 4000:4000 + EC].bitcast(I32)
        hid = kv_flat[:, 0:UN * FF].rearrange("p (u f) -> p u f", u=UN)

        ps = ctx.enter_context(nc.psum_tensor("ps", [P, 8, 512], F32))
        qd = [ps[:, 2 * b:2 * b + 2, :].rearrange("p b n -> p (b n)") for b in range(2)]
        agg = ps[:, 4:6, 0:MW]
        dst_rows = ps[:, 6:8, :].rearrange("p b n -> p (b n)")
        tp_all = ps[:, 5:7, :].rearrange("p b n -> p (b n)")[:, 0:UN * P].rearrange("p (u n) -> p u n", n=P)
        o_all = ps[:, 0:2, :].rearrange("p b n -> p (b n)")[:, 0:UN * D].rearrange("p (u n) -> p u n", n=D)
        wide = [ps[:, u, :] for u in range(UN)]
        cnt = ps[0:LO, 4, 0:HI]

        kv_tab = [nc.dram_tensor(f"kv_tab{l}", [NT * P, 2 * D], F32) for l in range(L)]

        rows_clear = sem("rows_clear")
        consts = sem("consts")
        edges_in = sem("edges_in")
        x_clear = sem("x_clear")
        x_in = sem("x_in")
        w_in = sems("w_in")
        chain = sem("chain")
        src_rows = sem("src_rows")
        src_T = sem("src_T")
        dst_T = sem("dst_T")
        hot_ready = sem("hot_ready")
        hot_used = sem("hot_used")
        npair_ready = sem("npair_ready")
        pair_ps = sem("pair_ps")
        tab_ready = sem("tab_ready")
        sq_ready = sem("sq_ready")
        sq_sum = sem("sq_sum")
        deg_sd = sem("deg_sd")
        f_pos = sem("f_pos")
        f_posT = sem("f_posT")
        f_posTc = sem("f_posTc")
        f_w = sem("f_w")
        f_bc = sem("f_bc")
        f_b = sem("f_b")
        f_done = sem("f_done")
        st_done = sems("st_done", 2 * L + 1)
        mv_done = sem("mv_done")
        sd_done = sem("sd_done")
        rstd_done = sem("rstd_done")
        nmr_done = sem("nmr_done")
        z_done = sems("z_done", 2 * L)
        tp_done = sems("tp_done", 2 * L)
        zT_done = sems("zT_done", 2 * L)
        qkv_ps = sems("qkv_ps")
        qkv_deg = sems("qkv_deg")
        qkv_done = sems("qkv_done")
        tab_out = sems("tab_out")
        q_part = sems("q_part", 5)
        self_prod = sem("self_prod")
        self_dot = sem("self_dot")
        self_mask = sem("self_mask")
        self_att = sem("self_att")
        self_exp = sem("self_exp")
        self_msg = sem("self_msg")
        idx_ready = sems("idx_ready")
        kv_in = [sems(f"kv_in{l}_", SLOTS) for l in range(L)]
        row_ready = sems("row_ready")
        dist_done = sems("dist_done")
        hotT_ready = sems("hotT_ready")
        hotT_used = sems("hotT_used")
        prod_done = sems("prod_done")
        dot_done = sems("dot_done")
        mask_done = sems("mask_done")
        att_done = sems("att_done")
        exp_done = sems("exp_done")
        msg_done = sems("msg_done")
        gathering = sems("gathering")
        hot_done = sems("hot_done")
        agg_done = sems("agg_done")
        evac_done = sems("evac_done")
        rs_done = sems("rs_done")
        ag_done = sems("ag_done")
        agT_ps = sems("agT_ps")
        agT_done = sems("agT_done")
        o_ps = sems("o_ps")
        x2_done = sems("x2_done")
        h_ps = sems("h_ps")
        h_done = sems("h_done")
        y_ps = sems("y_ps")
        y_b = sems("y_b")
        x3_done = sems("x3_done")
        first_in = sem("first_in")
        fin_add = sem("fin_add")
        fin_z = sem("fin_z")
        out_done = sem("out_done")

        block = ctx.enter_context(nc.Block())
        NCONST = 11
        NW = 23

        def load_pairs(eng, g):
            a = eng.value_load(pair_tab[0:1, 0, bass.ds(g, 1)], min_val=0, max_val=MAXPAIRS)
            b = eng.value_load(pair_tab[0:1, 1, bass.ds(g, 1)], min_val=1, max_val=MAXPAIRS)
            return a, b

        def load_shift(eng, g):
            return eng.value_load(pair_tab[0:1, 2, bass.ds(g, 1)], min_val=1, max_val=MAXPAIRS + TOFF)

        def tile_of(eng, pr, shift):
            return eng.snap((pr + TOFF - shift).with_bounds(min_val=0, max_val=NT - 1))

        def over_groups(eng, body):
            with eng.Fori(0, NG // SLOTS) as i:
                for u in range(SLOTS):
                    body(u, i, SLOTS * i + u)
            for u in range(NG % SLOTS):
                body(u, NG // SLOTS, NG // SLOTS * SLOTS + u)

        def over_tiles(eng, body):
            body(0)
            with eng.Fori(1, NU) as i:
                body(i)

        @block.sync
        def _(sp):
            sp.wait_ge(rows_clear, 2)
            for rows, d in ((src_i, src_d), (dst_i, dst_d)):
                sp.dma_start(rows[0:NG - 1, :], d[0:(NG - 1) * GE].rearrange("(g e) -> g e", e=GE)).then_inc(edges_in, 16)
                sp.dma_start(rows[NG - 1:NG, 0:ELAST], d[(NG - 1) * GE:E].rearrange("(g e) -> g e", g=1)).then_inc(edges_in, 16)
            sp.dma_start(x[:, 0:NT - 1, :], x_d[0:(NT - 1) * P, :].rearrange("(t p) d -> p t d", p=P)).then_inc(x_in, 16)
            sp.wait_ge(x_clear, 1)
            sp.dma_start(x[0:NLAST, NT - 1, :], x_d[(NT - 1) * P:N, :]).then_inc(x_in, 16)
            for l in range(L):
                if l:
                    sp.wait_ge(x3_done[l - 1], NT)
                    sp.wait_ge(y_ps[l - 1], NT)
                def load(to, what):
                    sp.dma_start(to, what).then_inc(w_in[l], 16)
                for n, k in enumerate(("Wq", "Wk", "Wv")):
                    load(wqkv[:, n * D:(n + 1) * D], W[k][l])
                load(wpos[:, :], W["Wpos"][l])
                load(wo[:, :], W["Wo"][l])
                load(w1[:, :], W["W1"][l])
                load(w2[:, :, :], W["W2"][l].rearrange("(c p) n -> p c n", p=P))
                for n, k in enumerate(("ln1_g", "ln1_b", "ln2_g", "ln2_b", "bpos", "bdeg")):
                    load(vecs[:, n:n + 1], W[k][l:l + 1, :].rearrange("a p -> p a"))
                load(wdeg_col[:, :], W["Wdeg"][l].rearrange("a p -> p a"))
                for c in range(FC):
                    load(b1_col[:, c:c + 1], W["b1"][l:l + 1, c * P:(c + 1) * P].rearrange("a p -> p a"))
                for n, k in enumerate(("bq", "bk", "bv")):
                    load(bqkv_bc[:, n * D:(n + 1) * D], W[k][l, :].partition_broadcast(P))
                load(bo_bc[:, :], W["bo"][l, :].partition_broadcast(P))
                load(b2_bc[:, :], W["b2"][l, :].partition_broadcast(P))
                table = kv_tab[l][:, :].rearrange("(t p) d -> p t d", p=P)
                with sp.Fori(0, NU) as i:
                    sp.wait_ge(qkv_done[l], UN * i + UN)
                    sp.dma_start(table[:, bass.ds(UN * i, UN), :], qkv[:, bass.ds(UN * i, UN), D:3 * D]).then_inc(tab_out[l], 16)
            sp.wait_ge(self_msg, L * NU)
            sp.wait_ge(q_part[4], L * NU)
            sp.wait_ge(tab_out[L - 1], 16 * NU)
            sp.dma_start(x_first[:, 0:NT - 1, :], x_d[0:(NT - 1) * P, :].rearrange("(t p) d -> p t d", p=P)).then_inc(first_in, 16)
            sp.dma_start(x_first[0:NLAST, NT - 1, :], x_d[(NT - 1) * P:N, :]).then_inc(first_in, 16)
            with sp.Fori(0, NU - 1) as i:
                sp.wait_ge(fin_z, UN * i + UN)
                sp.dma_start(out_d[bass.ds(UN * P * i, UN * P), :].rearrange("(t p) d -> p t d", p=P),
                             x[:, bass.ds(UN * i, UN), :]).then_inc(out_done, 16)
            sp.wait_ge(fin_z, NT)
            sp.dma_start(out_d[(NT - UN) * P:(NT - 1) * P, :].rearrange("(t p) d -> p t d", p=P),
                         x[:, NT - UN:NT - 1, :]).then_inc(out_done, 16)
            sp.dma_start(out_d[(NT - 1) * P:N, :], x[0:NLAST, NT - 1, :]).then_inc(out_done, 16)
            sp.wait_ge(out_done, 16 * (NU + 1))

        @block.gpsimd
        def _(pool):
            pool.memset(src_i, -1).then_inc(rows_clear, 1)
            pool.memset(dst_i, -1).then_inc(rows_clear, 1)
            pool.memset(x[:, NT - 1, :], 0.0).then_inc(x_clear, 1)
            pool.memset(ident[:, :], 0.0).then_inc(consts, 1)
            pool.wait_ge(consts, 1)
            pool.affine_select(out=ident[:, :], in_=ident[:, :], compare_op=ALU.not_equal, fill=1.0, base=0,
                               pattern=[[-1, P]], channel_multiplier=1).then_inc(consts, 1)
            pool.iota(lo_ref, pattern=[[1, LO], [0, HB]], base=0, channel_multiplier=0,
                      allow_small_or_imprecise_dtypes=True).then_inc(consts, 1)
            pool.iota(hi_ref, pattern=[[1, HI], [0, HB]], base=0, channel_multiplier=0,
                      allow_small_or_imprecise_dtypes=True).then_inc(consts, 1)
            pool.memset(ones[:, :], 1.0).then_inc(consts, 1)
            pool.memset(is_node[:, :], 1.0).then_inc(consts, 1)
            pool.memset(zeros[:, :], 0.0).then_inc(consts, 1)
            pool.wait_ge(consts, 7)
            pool.affine_select(out=is_node[:, :], in_=is_node[:, :], compare_op=ALU.is_ge, fill=0.0, base=N - 1,
                               pattern=[[-P, NT]], channel_multiplier=-1).then_inc(consts, 1)
            pool.affine_select(out=below[:, :], in_=ones[0:NG, 0:NG], compare_op=ALU.is_ge, fill=0.0, base=-1,
                               pattern=[[1, NG]], channel_multiplier=-1).then_inc(consts, 1)
            pool.iota(neg_node[:, :], pattern=[[-P, NT]], base=0, channel_multiplier=-1,
                      allow_small_or_imprecise_dtypes=True).then_inc(consts, 1)
            pool.iota(node_row[:, :], pattern=[[1, NT * P]], base=0, channel_multiplier=0,
                      allow_small_or_imprecise_dtypes=True).then_inc(consts, 1)
            pool.memset(row_pick[:, :, :], 0.0).then_inc(x_clear, 1)
            pool.wait_ge(x_clear, 2)
            pool.affine_select(out=row_pick[:, :, :], in_=row_pick[:, :, :], compare_op=ALU.not_equal, fill=1.0, base=0,
                               pattern=[[-1, NG], [0, P]], channel_multiplier=1).then_inc(x_clear, 1)

            for l in range(L):
                pool.wait_ge(tab_out[l], 16 * NU)

                def gather(u, i, g, first=False):
                    pool.wait_ge(idx_ready[l], g + 1)
                    if not first:
                        pool.wait_ge(msg_done[l], g - SLOTS + 1)
                    pool.sem_inc(gathering[l], 1)
                    for c in range(GC):
                        pool.indirect_dma_start(kv[:, u, c, :], None, kv_tab[l][:, :],
                                                bass.IndirectOffsetOnAxis(ap=idx[:, u, c:c + 1], axis=0)).then_inc(kv_in[l][u], 16)

                for u in range(SLOTS):
                    gather(u, 0, u, first=True)
                with pool.Fori(1, NG // SLOTS) as i:
                    for u in range(SLOTS):
                        gather(u, i, SLOTS * i + u)
                for u in range(NG % SLOTS):
                    gather(u, NG // SLOTS, NG // SLOTS * SLOTS + u)

        @block.scalar
        def _(act):
            def stats_sd(k, tiles_=slice(0, NT)):
                act.wait_ge(mv_done, 3 * k + 3)
                nc.scalar.activation(sd[:, :], var[:, :], ACT.Sqrt, bias=eps_col[:, :]).then_inc(sd_done, 1)

            def normalise(k, i, u, wait=True):
                t = UN * i + u
                if not (isinstance(i, int) and i == 0):
                    act.wait_ge(tp_done[k], i)
                nc.scalar.activation(z[:, u, :], x[:, t, :] if isinstance(t, int) else x[:, bass.ds(t, 1), :],
                                     ACT.Identity, bias=nmr[:, bass.ds(t, 1)], scale=rstd[:, bass.ds(t, 1)]).then_inc(z_done[k], 1)

            act.wait_ge(sq_sum, 1)
            nc.scalar.activation(dcol[:, 1:2], ps[:, 7, 0:1], ACT.Sqrt, scale=1.0 / (N - 1)).then_inc(deg_sd, 1)

            for l in range(L):
                stats_sd(2 * l)
                act.wait_ge(nmr_done, 2 * l + 1)

                def qkv_tiles(i):
                    for u in range(UN):
                        normalise(2 * l, i, u)
                over_tiles(act, qkv_tiles)
                with act.Fori(0, NU) as i:
                    block_ = bass.ds(UN * i, UN)
                    act.wait_ge(qkv_done[l], UN * i + UN)
                    nc.scalar.activation(q_parts[:, block_, 0:D], qkv[:, block_, 0:D], ACT.Copy).then_inc(q_part[0], 1)
                with act.Fori(0, NU) as i:
                    act.wait_ge(self_att, l * NU + i + 1)
                    nc.scalar.activation(acc[:, bass.ds(UN * i, UN), D:MW],
                                         att[:, 0:UN * H].rearrange("p (t h) -> p t h", h=H), ACT.Exp,
                                         scale=1.0 / SCALE).then_inc(self_exp, 1)
                act.sem_inc(hotT_used[l], 2)
                act.sem_inc(hotT_ready[l], 1)
                if l == 0:
                    act.wait_ge(tab_ready, 1)

                def one_hots(g):
                    a, b = load_pairs(act, g)
                    shift = load_shift(act, g)
                    act.wait_ge(row_ready[l], g + 1)
                    with act.Fori(a, b) as pr:
                        t = tile_of(act, pr, shift)
                        act.wait_ge(hotT_ready[l], pr + 1)
                        nc.scalar.activation(dist[:, :], dst_rows, ACT.Abs, bias=neg_node[:, bass.ds(t, 1)]).then_inc(dist_done[l], 1)
                        act.wait_ge(dist_done[l], pr + 1)
                        act.wait_ge(hotT_used[l], pr + 1)
                        nc.scalar.activation(hotT[:, bass.ds(pr % 2, 1), :], dist[:, :], ACT.Relu, bias=1.0, scale=-1.0).then_inc(hotT_ready[l], 1)

                def weights(g):
                    a = act.value_load(pair_tab[0:1, 0, bass.ds(g, 1)], min_val=0, max_val=MAXPAIRS)
                    act.wait_ge(att_done[l], g + 1)
                    act.wait_ge(agg_done[l], a + 1)
                    nc.scalar.activation(msg[:, :, D:MW], att[:, :].rearrange("p (c h) -> p c h", h=H), ACT.Exp,
                                         scale=1.0 / SCALE).then_inc(exp_done[l], 1)

                one_hots(0)
                one_hots(1)
                with act.Fori(0, NG // SLOTS) as i:
                    for u in range(SLOTS):
                        weights(SLOTS * i + u)
                        one_hots(SLOTS * i + u + 2)
                weights(NG - 2)
                weights(NG - 1)
                stats_sd(2 * l + 1)
                act.wait_ge(nmr_done, 2 * l + 1 + 1)

                def ffn_tiles(i):
                    for u in range(UN):
                        normalise(2 * l + 1, i, u)
                    for u in range(UN):
                        act.wait_ge(h_ps[l], UN * i + u + 1)
                        for c in range(FC):
                            last = nc.scalar.activation(hid[:, u, c * P:(c + 1) * P], wide[u][:, c * P:(c + 1) * P], ACT.Gelu,
                                                        bias=b1f[:, c:c + 1])
                        last.then_inc(h_done[l], 1)
                over_tiles(act, ffn_tiles)
            stats_sd(2 * L)
            act.wait_ge(nmr_done, 2 * L + 1)
            with act.Fori(0, NT) as t:
                nc.scalar.activation(x[:, bass.ds(t, 1), :], x[:, bass.ds(t, 1), :], ACT.Identity,
                                     bias=nmr[:, bass.ds(t, 1)], scale=rstd[:, bass.ds(t, 1)]).then_inc(fin_z, 1)

        @block.vector
        def _(dve):
            links = [0]

            def link(ins):
                links[0] += 1
                ins.then_inc(chain, 1)
                dve.wait_ge(chain, links[0])

            def tile_stats(k, t, ready):
                nc.vector.bn_stats(stats[:, bass.ds(t, 1), :], x[:, bass.ds(t, 1), :]).then_inc(st_done[k], 1)

            def all_stats(k):
                dve.wait_ge(st_done[k], NT)
                nc.vector.tensor_tensor(half_gap[:, :], stats[:, :, 1], stats[:, :, 4], ALU.subtract)
                nc.vector.tensor_tensor(mean2[:, :], stats[:, :, 1], stats[:, :, 4], ALU.add)
                nc.vector.tensor_tensor(sq_dev[:, :], stats[:, :, 2], stats[:, :, 5], ALU.add).then_inc(mv_done, 1)
                dve.wait_ge(mv_done, 3 * k + 1)
                nc.vector.scalar_tensor_tensor(out=gap2[:, :], in0=half_gap[:, :], scalar=0.25, in1=half_gap[:, :],
                                               op0=ALU.mult, op1=ALU.mult).then_inc(mv_done, 1)
                dve.wait_ge(mv_done, 3 * k + 2)
                nc.vector.scalar_tensor_tensor(out=var[:, :], in0=sq_dev[:, :], scalar=1.0 / D, in1=gap2[:, :],
                                               op0=ALU.mult, op1=ALU.add).then_inc(mv_done, 1)
                dve.wait_ge(sd_done, k + 1)
                nc.vector.reciprocal(rstd[:, :], sd[:, :]).then_inc(rstd_done, 1)
                dve.wait_ge(rstd_done, k + 1)
                nc.vector.scalar_tensor_tensor(out=nmr[:, :], in0=mean2[:, :], scalar=-0.5, in1=rstd[:, :],
                                               op0=ALU.mult, op1=ALU.mult).then_inc(nmr_done, 1)

            link(nc.vector.memset(eps_col[:, :], EPS))
            link(nc.vector.memset(dev[:, :], 0.0))
            dve.wait_ge(edges_in, 64)
            nc.vector.tensor_copy(src_f, src_i).then_inc(src_rows, 1)
            nc.vector.tensor_copy(dst_f, dst_i).then_inc(src_rows, 1)
            link(nc.vector.tensor_single_scalar(tmp_i, dst_i, 7, ALU.arith_shift_right))
            link(nc.vector.tensor_single_scalar(tmp_j, dst_i, P - 1, ALU.bitwise_and))
            link(nc.vector.tensor_scalar(dst_hi[:, :], tmp_i, float(P), None, ALU.mult))
            link(nc.vector.tensor_copy(dst_lo[:, :], tmp_j))
            def cols(bank):
                return ps[:, bank:bank + 2, 0:4 * NG]
            dve.wait_ge(src_T, 1)
            link(nc.vector.tensor_scalar(src_idx[:, :, :].rearrange("p (b c) g -> p b (c g)", b=2), cols(0), 0.0, None, ALU.max))
            link(nc.vector.tensor_copy(src_ci.rearrange("p (b n) -> p b n", b=2), cols(0)))
            link(nc.vector.tensor_single_scalar(lo_i, src_ci, LO - 1, ALU.bitwise_and))
            link(nc.vector.tensor_single_scalar(hi_i, src_ci, LO.bit_length() - 1, ALU.arith_shift_right))
            link(nc.vector.tensor_copy(src_lo, lo_i))
            link(nc.vector.tensor_copy(src_hi, hi_i))
            dve.wait_ge(consts, 4)
            with dve.Fori(0, NHB // 2) as i:
                for b in range(2):
                    k = 2 * i + b
                    dve.wait_ge(hot_used, k + 1)
                    nc.vector.tensor_tensor(hot_lo[b], lo_ref, spread(src_lo[:, bass.ds(k * HB, HB)], 1, LO), ALU.is_equal)
                    nc.vector.tensor_tensor(hot_hi[b], hi_ref, spread(src_hi[:, bass.ds(k * HB, HB)], 1, HI), ALU.is_equal).then_inc(hot_ready, 1)
            dve.wait_ge(dst_T, 1)
            link(nc.vector.tensor_copy(dst_col[:, :, :].rearrange("p (b c) g -> p b (c g)", b=2), cols(2)))
            dve.wait_ge(src_rows, 2)
            link(nc.vector.tensor_scalar(tmp_f, dst_f, 0.0, float(2 * NT * P), ALU.is_lt, ALU.mult))
            link(nc.vector.tensor_tensor(tmp_f, tmp_f, dst_f, ALU.add))
            link(nc.vector.tensor_reduce(ext[:, 0:1], tmp_f, AX.X, ALU.min))
            link(nc.vector.tensor_reduce(ext[:, 1:2], dst_f, AX.X, ALU.max))
            link(nc.vector.tensor_copy(ext_i[:, :], ext[:, :]))
            link(nc.vector.tensor_single_scalar(ext_t[:, :], ext_i[:, :], 7, ALU.arith_shift_right))
            link(nc.vector.tensor_copy(tiles[:, :], ext_t[:, :]))
            nc.vector.scalar_tensor_tensor(out=npair[:, :], in0=tiles[:, 1:2], scalar=1.0, in1=tiles[:, 0:1],
                                           op0=ALU.add, op1=ALU.subtract).then_inc(npair_ready, 1)
            dve.wait_ge(pair_ps, 1)
            first_ps, count_ps, tile_ps = (ps[0:1, 7, 128 * k:128 * k + NG] for k in (1, 2, 3))
            link(nc.vector.tensor_copy(pair_f[:, 0, :], first_ps))
            link(nc.vector.tensor_tensor(pair_f[:, 1, :], pair_f[:, 0, :], count_ps, ALU.add))
            link(nc.vector.scalar_tensor_tensor(out=pair_f[:, 2, :], in0=pair_f[:, 0, :], scalar=float(TOFF), in1=tile_ps,
                                                op0=ALU.add, op1=ALU.subtract))
            nc.vector.tensor_copy(pair_tab[:, :, :], pair_f[:, :, :]).then_inc(tab_ready, 1)
            dve.wait_ge(hot_used, NHB + 2)
            dve.wait_ge(consts, NCONST)
            link(nc.vector.tensor_copy(dev[0:LO, 0:NT], cnt[:, 0:HI:2]))
            link(nc.vector.tensor_copy(dev[LO:2 * LO, 0:HI // 2], cnt[:, 1:HI:2]))
            link(nc.vector.scalar_tensor_tensor(out=dev[:, :], in0=dev[:, :], scalar=1.0 - MEAN_DEG, in1=is_node[:, :],
                                                op0=ALU.add, op1=ALU.mult))
            link(nc.vector.tensor_tensor(dev2[:, :], dev[:, :], dev[:, :], ALU.mult))
            nc.vector.tensor_reduce(dcol[:, 0:1], dev2[:, :], AX.X, ALU.add).then_inc(sq_ready, 1)
            dve.wait_ge(deg_sd, 1)
            link(nc.vector.tensor_scalar(dcol[:, 2:3], dcol[:, 1:2], 1e-6, None, ALU.add))
            link(nc.vector.reciprocal(dcol[:, 3:4], dcol[:, 2:3]))
            link(nc.vector.tensor_scalar(degn[:, :], dev[:, :], dcol[:, 3:4], None, ALU.mult))

            for l in range(L):
                dve.wait_ge(w_in[l], 16 * NW)
                nc.vector.tensor_tensor(pos1[:, :], wpos[:, :], ident[:, :], ALU.add).then_inc(f_pos, 1)
                dve.wait_ge(f_posT, l + 1)
                nc.vector.tensor_copy(posT[:, :], ps[:, 7, 0:P]).then_inc(f_posTc, 1)
                link(nc.vector.tensor_tensor(cvec[:, 0:1], vecs[:, 4:5], vecs[:, 5:6], ALU.add))
                link(nc.vector.tensor_tensor(cvec[:, 1:2], cvec[:, 0:1], ps[:, 7, P:P + 1], ALU.add))
                link(nc.vector.tensor_scalar(c_bc[:, :], ones[:, :], cvec[:, 1:2], None, ALU.mult))
                nc.vector.tensor_scalar(wd_bc[:, :], ones[:, :], wdeg_col[:, 0:1], None, ALU.mult).then_inc(f_bc, 1)
                nc.vector.tensor_scalar(w1g[:, :], w1[:, :], vecs[:, 2:3], None, ALU.mult)
                dve.wait_ge(f_w, l + 1)
                nc.vector.tensor_scalar(wfold[:, :], ps[:, 0, 0:3 * D], vecs[:, 0:1], None, ALU.mult)
                dve.wait_ge(f_b, l + 1)
                nc.vector.tensor_tensor(bfold[:, :], bqkv_bc[:, :], ps[:, 1, 0:3 * D], ALU.add)
                nc.vector.tensor_copy(degw[:, :], ps[:, 2, 0:3 * D])
                nc.vector.tensor_tensor(b1f[:, :], b1_col[:, :], ps[:, 3, 0:FC], ALU.add).then_inc(f_done, 1)
                dve.wait_ge(f_done, l + 1)
                if l == 0:
                    dve.wait_ge(x_in, 32)
                    with dve.Fori(0, NT) as t:
                        tile_stats(0, t, None)
                all_stats(2 * l)

                def qkv_tiles(i):
                    dve.wait_ge(tp_done[2 * l], i + 1)
                    nc.vector.tensor_copy(zT[:, :, :], tp_all).then_inc(zT_done[2 * l], 1)
                    for u in range(UN):
                        t = UN * i + u
                        dve.wait_ge(qkv_ps[l], t + 1)
                        nc.vector.scalar_tensor_tensor(out=qkv[:, bass.ds(t, 1), :], in0=degw[:, :].unsqueeze(1), scalar=degn[:, bass.ds(t, 1)],
                                                       in1=wide[u][:, 0:3 * D].unsqueeze(1), op0=ALU.mult, op1=ALU.add).then_inc(qkv_deg[l], 1)
                        dve.wait_ge(qkv_deg[l], t + 1)
                        nc.vector.tensor_tensor(qkv[:, bass.ds(t, 1), :], qkv[:, bass.ds(t, 1), :], bfold[:, :].unsqueeze(1), ALU.add).then_inc(qkv_done[l], 1)
                over_tiles(dve, qkv_tiles)

                def fetch_idx(u, g):
                    nc.vector.tensor_copy(idx[:, u, :], src_idx[:, :, bass.ds(g, 1)].rearrange("p c o -> p (c o)")).then_inc(idx_ready[l], 1)
                for u in range(SLOTS):
                    fetch_idx(u, u)

                with dve.Fori(0, NU) as i:
                    tb = bass.ds(UN * i, UN)
                    rest = prod[:, 0:UN * D].rearrange("p (t d) -> p t d", d=D)
                    dve.wait_ge(qkv_done[l], UN * i + UN)
                    dve.wait_ge(q_part[0], l * NU + i + 1)
                    nc.vector.tensor_tensor(rest, qkv[:, tb, 0:D], q_parts[:, tb, 0:D], ALU.subtract).then_inc(q_part[1], 1)
                    dve.wait_ge(q_part[1], l * NU + i + 1)
                    nc.vector.tensor_copy(q_parts[:, tb, D:2 * D], rest).then_inc(q_part[2], 1)
                    dve.wait_ge(q_part[2], l * NU + i + 1)
                    nc.vector.tensor_tensor(rest, rest, q_parts[:, tb, D:2 * D], ALU.subtract).then_inc(q_part[3], 1)
                    dve.wait_ge(q_part[3], l * NU + i + 1)
                    nc.vector.tensor_copy(q_parts[:, tb, 2 * D:3 * D], rest).then_inc(q_part[4], 1)
                    dve.wait_ge(q_part[4], l * NU + i + 1)
                    n = UN * H
                    nc.vector.tensor_tensor(rest, qkv[:, tb, 0:D], qkv[:, tb, D:2 * D], ALU.mult).then_inc(self_prod, 1)
                    dve.wait_ge(self_prod, l * NU + i + 1)
                    nc.vector.tensor_reduce(dots[:, 0:n], prod[:, 0:UN * D].rearrange("p (n d) -> p n d", d=HD), AX.X, ALU.add).then_inc(self_dot, 1)
                    dve.wait_ge(self_dot, l * NU + i + 1)
                    nc.vector.tensor_tensor(not_nan[:, 0:n], dots[:, 0:n], dots[:, 0:n], ALU.is_equal)
                    nc.vector.tensor_scalar(clipped[:, 0:n], dots[:, 0:n], CLIP * SCALE, -CLIP * SCALE, ALU.min, ALU.max).then_inc(self_mask, 1)
                    dve.wait_ge(self_mask, l * NU + i + 1)
                    nc.vector.tensor_tensor(att[:, 0:n], clipped[:, 0:n], not_nan[:, 0:n], ALU.mult).then_inc(self_att, 1)
                    dve.wait_ge(self_exp, l * NU + i + 1)
                    nc.vector.tensor_tensor(acc[:, tb, 0:D].rearrange("p t (h d) -> p t h d", d=HD),
                                            qkv[:, tb, 2 * D:3 * D].rearrange("p t (h d) -> p t h d", d=HD),
                                            spread(acc[:, tb, D:MW], 3, HD), ALU.mult).then_inc(self_msg, 1)
                dve.wait_ge(self_msg, l * NU + NU)
                nc.vector.tensor_tensor(x[:, :, :], x[:, :, :], spread(bo_bc[:, :], 1, NT), ALU.add)

                prev_tile = dve.alloc_register(f"prev_tile{l}")
                dve.reg_mov(prev_tile, 0)
                nc.vector.memset(agg[:, 1, :], 0.0).then_inc(agg_done[l], 1)
                dve.sem_inc(evac_done[l], 1)

                def evacuate(pr_plus_1):
                    t = dve.snap(prev_tile, min_val=0, max_val=NT - 1)
                    dve.wait_ge(agg_done[l], pr_plus_1)
                    dve.wait_ge(evac_done[l], pr_plus_1)
                    nc.vector.tensor_tensor(acc[:, bass.ds(t, 1), :], acc[:, bass.ds(t, 1), :],
                                            agg[:, bass.ds(pr_plus_1 % 2, 1), :], ALU.add).then_inc(evac_done[l], 1)

                def edge_group(u, i, g, fetch=True):
                    a, b = load_pairs(dve, g)
                    shift = load_shift(dve, g)
                    dve.wait_ge(kv_in[l][u], 16 * GC * (i + 1))
                    dve.wait_ge(hotT_used[l], b + 2)
                    nc.vector.tensor_tensor(prod[:, :].rearrange("p (c d) -> p c d", d=D), kv[:, u, :, 0:D],
                                            qd[u % 2].rearrange("p (c d) -> p c d", d=D), ALU.mult).then_inc(prod_done[l], 1)
                    if fetch:
                        fetch_idx(u, g + SLOTS)
                    dve.wait_ge(prod_done[l], g + 1)
                    nc.vector.tensor_reduce(dots[:, :], prod[:, :].rearrange("p (n d) -> p n d", d=HD), AX.X, ALU.add).then_inc(dot_done[l], 1)
                    dve.wait_ge(dot_done[l], g + 1)
                    nc.vector.tensor_tensor(not_nan[:, :], dots[:, :], dots[:, :], ALU.is_equal)
                    nc.vector.tensor_scalar(clipped[:, :], dots[:, :], CLIP * SCALE, -CLIP * SCALE, ALU.min, ALU.max).then_inc(mask_done[l], 1)
                    dve.wait_ge(mask_done[l], g + 1)
                    nc.vector.tensor_tensor(att[:, :], clipped[:, :], not_nan[:, :], ALU.mult).then_inc(att_done[l], 1)
                    dve.wait_ge(exp_done[l], g + 1)
                    nc.vector.tensor_tensor(msg[:, :, 0:D].rearrange("p c (h d) -> p c h d", d=HD),
                                            kv[:, u, :, D:2 * D].rearrange("p c (h d) -> p c h d", d=HD),
                                            spread(msg[:, :, D:MW], 3, HD), ALU.mult).then_inc(msg_done[l], 1)
                    with dve.Fori(a, b) as pr:
                        t = tile_of(dve, pr, shift)
                        dve.wait_ge(agg_done[l], pr + 1)
                        nc.vector.tensor_tensor(hot[:, :, :], spread(node_row[:, bass.ds(t * P, P)], 1, GC),
                                                dst_col[:, :, bass.ds(g, 1)].broadcast_to([P, GC, P]), ALU.is_equal).then_inc(hot_done[l], 1)
                        evacuate(pr + 1)
                        dve.reg_mov(prev_tile, t)

                with dve.Fori(0, NG // SLOTS - 1) as i:
                    for u in range(SLOTS):
                        edge_group(u, i, SLOTS * i + u)
                for g in range((NG // SLOTS - 1) * SLOTS, NG):
                    edge_group(g % SLOTS, g // SLOTS, g, fetch=g + SLOTS < NG)
                end = dve.value_load(pair_tab[0:1, 1, NG - 1:NG], min_val=1, max_val=MAXPAIRS)
                evacuate(end + 1)
                dve.wait_ge(evac_done[l], end + 2)

                def out_tiles(i):
                    tb = bass.ds(UN * i, UN)
                    nc.vector.reciprocal(rsum[:, :, :], acc[:, tb, D:MW]).then_inc(rs_done[l], 1)
                    dve.wait_ge(rs_done[l], i + 1)
                    nc.vector.tensor_tensor(z[:, :, :].rearrange("p t (h d) -> p t h d", d=HD),
                                            acc[:, tb, 0:D].rearrange("p t (h d) -> p t h d", d=HD),
                                            spread(rsum[:, :, :], 3, HD), ALU.mult).then_inc(ag_done[l], 1)
                    dve.wait_ge(agT_ps[l], i + 1)
                    nc.vector.tensor_copy(zT[:, :, :], tp_all).then_inc(agT_done[l], 1)
                    dve.wait_ge(o_ps[l], i + 1)
                    nc.vector.tensor_tensor(x[:, tb, :], x[:, tb, :], o_all, ALU.add).then_inc(x2_done[l], 1)
                    dve.wait_ge(x2_done[l], i + 1)
                    for u in range(UN):
                        tile_stats(2 * l + 1, UN * i + u, None)
                over_tiles(dve, out_tiles)
                all_stats(2 * l + 1)

                def ffn_tiles(i):
                    dve.wait_ge(tp_done[2 * l + 1], i + 1)
                    nc.vector.tensor_copy(zT[:, :, :], tp_all).then_inc(zT_done[2 * l + 1], 1)
                    for u in range(UN):
                        t = UN * i + u
                        dve.wait_ge(z_done[2 * l + 1], t + 1)
                        nc.vector.tensor_tensor(x[:, bass.ds(t, 1), :], x[:, bass.ds(t, 1), :], b2_bc[:, :].unsqueeze(1), ALU.add).then_inc(y_b[l], 1)
                        dve.wait_ge(y_ps[l], t + 1)
                        dve.wait_ge(y_b[l], t + 1)
                        nc.vector.tensor_tensor(x[:, bass.ds(t, 1), :], x[:, bass.ds(t, 1), :], wide[u][:, 0:D].unsqueeze(1), ALU.add).then_inc(x3_done[l], 1)
                        dve.wait_ge(x3_done[l], t + 1)
                        if l == L - 1:
                            if isinstance(i, int) and u == 0:
                                dve.wait_ge(first_in, 32)
                            nc.vector.tensor_tensor(x[:, bass.ds(t, 1), :], x[:, bass.ds(t, 1), :], x_first[:, bass.ds(t, 1), :], ALU.add).then_inc(fin_add, 1)
                            dve.wait_ge(fin_add, t + 1)
                        tile_stats(2 * l + 2, t, None)
                over_tiles(dve, ffn_tiles)
            all_stats(2 * L)

        @block.tensor
        def _(pe):
            MM = nc.tensor.matmul
            pe.sem_inc(hot_used, 2)
            pe.wait_ge(consts, 2)
            pe.wait_ge(src_rows, 2)
            for which, bank, done in ((src_f, 0, src_T), (dst_f, 2, dst_T)):
                for c in range(GC):
                    last = nc.tensor.transpose(ps[:, bank + c // 4, (c % 4) * NG:(c % 4 + 1) * NG], which[:, c * P:(c + 1) * P], ident[0:NG, 0:NG])
                last.then_inc(done, 1)
            pe.wait_ge(consts, 7)
            MM(cnt, zeros[:, 0:LO], zeros[:, 0:HI], start=True, stop=False, skip_group_check=True)
            with pe.Fori(0, NHB // 2) as i:
                for b in range(2):
                    k = 2 * i + b
                    pe.wait_ge(hot_ready, k + 1)
                    for c in range(HB):
                        last = MM(cnt, hot_lo[b][:, :, c], hot_hi[b][:, :, c], start=False, stop=True, skip_group_check=True)
                    last.then_inc(hot_used, 1)
            pe.wait_ge(npair_ready, 1)
            pe.wait_ge(consts, 9)
            MM(ps[0:1, 7, 128:128 + NG], npair[:, :], below[:, :], start=True, stop=True)
            MM(ps[0:1, 7, 256:256 + NG], npair[:, :], ident[0:NG, 0:NG], start=True, stop=True)
            MM(ps[0:1, 7, 384:384 + NG], tiles[:, 0:1], ident[0:NG, 0:NG], start=True, stop=True).then_inc(pair_ps, 1)
            pe.wait_ge(sq_ready, 1)
            MM(ps[:, 7, 0:1], ones[:, :], dcol[:, 0:1], start=True, stop=True).then_inc(sq_sum, 1)

            for l in range(L):
                pe.wait_ge(f_pos, l + 1)
                if l == 0:
                    pe.wait_ge(deg_sd, 1)
                nc.tensor.transpose(ps[:, 7, 0:P], pos1[:, :], ident[:, :])
                MM(ps[:, 7, P:P + 1], pos1[:, :], vecs[:, 1:2], start=True, stop=True).then_inc(f_posT, 1)
                pe.wait_ge(f_posTc, l + 1)
                MM(ps[:, 0, 0:3 * D], posT[:, :], wqkv[:, :], start=True, stop=True).then_inc(f_w, 1)
                pe.wait_ge(f_bc, l + 1)
                MM(ps[:, 1, 0:3 * D], c_bc[:, :], wqkv[:, :], start=True, stop=True)
                MM(ps[:, 2, 0:3 * D], wd_bc[:, :], wqkv[:, :], start=True, stop=True)
                for c in range(FC):
                    last = MM(ps[:, 3, c:c + 1], w1[:, c * P:(c + 1) * P], vecs[:, 3:4], start=True, stop=True)
                last.then_inc(f_b, 1)
                pe.wait_ge(f_done, l + 1)

                def transposed(k, i):
                    for u in range(UN):
                        pe.wait_ge(z_done[k], UN * i + u + 1)
                        last = nc.tensor.transpose(tp_all[:, u, :], z[:, u, :], ident[:, :])
                    last.then_inc(tp_done[k], 1)

                def qkv_tiles(i):
                    transposed(2 * l, i)
                    pe.wait_ge(zT_done[2 * l], i + 1)
                    for u in range(UN):
                        MM(wide[u][:, 0:3 * D], zT[:, u, :], wfold[:, :], start=True, stop=True).then_inc(qkv_ps[l], 1)
                over_tiles(pe, qkv_tiles)

                if l == 0:
                    pe.wait_ge(x_clear, 3)
                    pe.wait_ge(tab_ready, 1)
                pe.wait_ge(qkv_done[l], NT)
                pe.wait_ge(q_part[4], l * NU + NU)

                def broadcast_rows(g, a):
                    if a is not None:
                        pe.wait_ge(dist_done[l], a)
                    for half in range(2):
                        cut = slice(512 * half, 512 * half + 512)
                        for part, start in ((dst_hi, True), (dst_lo, False)):
                            last = MM(dst_rows[:, cut], row_pick[:, bass.ds(g, 1), :], part[:, cut], start=start, stop=not start)
                    last.then_inc(row_ready[l], 1)

                def gather_q(u, g, a, b):
                    shift = load_shift(pe, g)
                    if not (isinstance(g, int) and g < 2):
                        pe.wait_ge(prod_done[l], g - 1)
                    for half in range(2):
                        MM(qd[u % 2][:, 512 * half:512 * half + 512], zeros[:, 0:P], zeros[:, :], start=True, stop=False, skip_group_check=True)
                    with pe.Fori(a, b) as pr:
                        t = tile_of(pe, pr, shift)
                        pe.wait_ge(hotT_ready[l], pr + 2)
                        for c in range(GC):
                            for k in range(3):
                                last = MM(qd[u % 2][:, c * P:(c + 1) * P], hotT[:, bass.ds(pr % 2, 1), c * P:(c + 1) * P],
                                          q_parts[:, bass.ds(t, 1), k * D:(k + 1) * D], start=False, stop=True, skip_group_check=True)
                        last.then_inc(hotT_used[l], 1)

                def sum_messages(g, a, b):
                    with pe.Fori(a, b) as pr:
                        pe.wait_ge(msg_done[l], g + 1)
                        pe.wait_ge(hot_done[l], pr + 1)
                        pe.wait_ge(evac_done[l], pr + 1)
                        for c in range(GC):
                            last = MM(agg[:, bass.ds(pr % 2, 1), :], hot[:, c, :], msg[:, c, :], start=(c == 0), stop=(c == GC - 1))
                        last.then_inc(agg_done[l], 1)

                def pe_group(u, g, more=True, ahead=True):
                    if more:
                        gather_q(u + 1, g + 1, *load_pairs(pe, g + 1))
                    if ahead:
                        broadcast_rows(g + 2, load_pairs(pe, g + 2)[0])
                    sum_messages(g, *load_pairs(pe, g))

                broadcast_rows(0, None)
                gather_q(0, 0, *load_pairs(pe, 0))
                broadcast_rows(1, load_pairs(pe, 1)[0])
                pe_group_first = True
                gather_q(1, 1, *load_pairs(pe, 1))
                broadcast_rows(2, load_pairs(pe, 2)[0])
                sum_messages(0, *load_pairs(pe, 0))
                for g in range(1, SLOTS):
                    pe_group(g, g)
                with pe.Fori(1, NG // SLOTS) as i:
                    for u in range(SLOTS):
                        pe_group(u, SLOTS * i + u)
                pe_group(NG - 2, NG - 2, ahead=False)
                pe_group(NG - 1, NG - 1, more=False, ahead=False)

                def out_tiles(i):
                    pe.wait_ge(ag_done[l], i + 1)
                    for u in range(UN):
                        last = nc.tensor.transpose(tp_all[:, u, :], z[:, u, :], ident[:, :])
                    last.then_inc(agT_ps[l], 1)
                    pe.wait_ge(agT_done[l], i + 1)
                    for u in range(UN):
                        last = MM(o_all[:, u, :], zT[:, u, :], wo[:, :], start=True, stop=True)
                    last.then_inc(o_ps[l], 1)
                over_tiles(pe, out_tiles)

                def ffn_tiles(i):
                    transposed(2 * l + 1, i)
                    pe.wait_ge(zT_done[2 * l + 1], i + 1)
                    for u in range(UN):
                        for c in range(FC):
                            last = MM(wide[u][:, c * P:(c + 1) * P], w1g[:, c * P:(c + 1) * P], zT[:, u, :], start=True, stop=True)
                        last.then_inc(h_ps[l], 1)
                    for u in range(UN):
                        pe.wait_ge(h_done[l], UN * i + u + 1)
                        for c in range(FC):
                            last = MM(wide[u][:, 0:D], hid[:, u, c * P:(c + 1) * P], w2[:, c, :], start=(c == 0), stop=(c == FC - 1))
                        last.then_inc(y_ps[l], 1)
                over_tiles(pe, ffn_tiles)


_WEIGHTS = ["Wq", "bq", "Wk", "bk", "Wv", "bv", "Wo", "bo", "Wpos", "bpos", "Wdeg", "bdeg",
            "ln1_g", "ln1_b", "ln2_g", "ln2_b", "W1", "b1", "W2", "b2"]


def kernel(**inputs):
    import numpy as _np
    import concourse.bacc as _bacc
    from concourse import mybir as _mybir
    from concourse.bass_utils import run_bass_kernel_spmd as _run

    nc = _bacc.Bacc("TRN2", target_bir_lowering=False, num_devices=1)
    arrays = {}

    def given(name):
        a = _np.ascontiguousarray(inputs[name])
        arrays[f"in_{name}"] = a
        return nc.dram_tensor(f"in_{name}", a.shape, _mybir.dt.from_np(a.dtype), kind="ExternalInput").ap()

    x, src, dst = given("x"), given("src"), given("dst")
    weights = {k: given(f"L0_gnn_{k}") for k in _WEIGHTS}
    out = nc.dram_tensor("out_0", (N, D), _mybir.dt.float32, kind="ExternalOutput").ap()
    gnn_program(nc, x, src, dst, weights, out)
    r = _run(nc, [arrays], core_ids=[0])
    return r.results[0]["out_0"]
```

```python
import numpy as np
import concourse.bass as bass
from concourse import mybir
from contextlib import ExitStack

F32 = mybir.dt.float32
BF16 = mybir.dt.bfloat16
I32 = mybir.dt.int32
ALU = mybir.AluOpType
ACT = mybir.ActivationFunctionType
AX = mybir.AxisListType

N, E, D, H, L, FF = 3125, 100000, 128, 8, 2, 512
HD = D // H
P = 128
NT = -(-N // P)
NLAST = N - (NT - 1) * P
GC = 8
GE = GC * P
NG = -(-E // GE)
ELAST = E - (NG - 1) * GE
MW = D + H
SLOTS = 4
UN = 5
NU = NT // UN
FC = FF // P
LO = 64
HI = -(-N // LO)
HB = 28
NHB = NG * GC // HB
FOLD_AT = 4
EPS = 1e-5
CLIP = 50.0
SCALE = float(HD) ** 0.5
MEAN_DEG = (E + N) / N
TOFF = 32
MAXPAIRS = NG * NT
WORD_BITS = 12
WORD = 1 << WORD_BITS
assert MAXPAIRS + TOFF < WORD and MAXPAIRS * WORD < 1 << 24
assert NT % UN == 0 and NHB * HB == NG * GC and NHB % 2 == 0 and NG % SLOTS == 2


def gnn_program(nc, x_d, src_d, dst_d, W, out_d):
    ctx = ExitStack()
    with ctx:
        def sb(name, shape, dt=F32):
            return ctx.enter_context(nc.sbuf_tensor(name, shape, dt))

        def sem(name):
            return ctx.enter_context(nc.semaphore(name))

        def spread(ap, axis, n):
            new = ap.unsqueeze(axis)
            shape = list(new.shape)
            shape[axis] = n
            return new.broadcast_to(shape)

        def sems(name, n=L):
            return [sem(f"{name}{i}") for i in range(n)]

        x = sb("x", [P, NT, D])
        qkv = sb("qkv", [P, NT, 3 * D])
        q_parts = sb("q_parts", [P, NT, 3 * D], BF16)
        acc = sb("acc", [P, NT, MW])
        x_first = qkv[:, :, 0:D]
        kv = sb("kv", [P, SLOTS, GC, 2 * D])
        dst_hi = sb("dst_hi", [NG, GE], BF16)
        dst_lo = sb("dst_lo", [NG, GE], BF16)
        dst_col = sb("dst_col", [P, GC, NG])
        src_idx = sb("src_idx", [P, GC, NG], I32)
        idx = sb("idx", [P, SLOTS, GC], I32)
        pair_tab = sb("pair_tab", [1, NG + 2], I32)
        dist = sb("dist", [P, GE], BF16)
        hotT = sb("hotT", [P, 2, GE], BF16)
        hot = sb("hot", [P, 2, GC, P])
        prod = sb("prod", [P, GE])
        dots = sb("dots", [P, GC * H])
        not_nan = sb("not_nan", [P, GC * H])
        clipped = sb("clipped", [P, GC * H])
        att = sb("att", [P, GC * H])
        msg = sb("msg", [P, 2, GC, MW])
        pick = sb("pick", [NG, 2, P], BF16)
        ident = sb("ident", [P, P])
        ones = sb("ones", [P, P])
        zeros = sb("zeros", [P, 512], BF16)
        below = sb("below", [NG, NG])
        node_row = sb("node_row", [P, NT * P])
        neg_node = sb("neg_node", [P, NT])
        is_node = sb("is_node", [P, NT])
        eps_col = sb("eps_col", [P, 1])
        wfold = sb("wfold", [P, L, 3 * D])
        bfold = sb("bfold", [P, L, 3 * D])
        degw = sb("degw", [P, L, 3 * D])
        wo = sb("wo", [P, L, D])
        w1g = sb("w1g", [P, L, FF])
        b1f = sb("b1f", [P, L, FC])
        w2 = sb("w2", [P, L, FC, D])
        bo_bc = sb("bo_bc", [P, L, D])
        b2_bc = sb("b2_bc", [P, L, D])
        vecs = sb("vecs", [P, L, 7])
        cvec = sb("cvec", [P, 2])
        posT, pos1, c_bc, wd_bc = (hot[:, 0, k, :] for k in range(4))
        raw = hot[:, 1, :, :].rearrange("p c n -> p (c n)")
        wqkv, wpos, w1 = raw[:, 0:3 * D], raw[:, 3 * D:4 * D], raw[:, 4 * D:4 * D + FF]
        raw_rows = msg[:, 1, :, :].rearrange("p c n -> p (c n)")
        bqkv_row, b1_row = raw_rows[0:1, 0:3 * D], raw_rows[0:1, 3 * D:3 * D + FF]
        stats = sb("stats", [P, NT, 6])
        half_gap = sb("half_gap", [P, NT])
        mean2 = sb("mean2", [P, NT])
        sq_dev = sb("sq_dev", [P, NT])
        gap2 = sb("gap2", [P, NT])
        var = sb("var", [P, NT])
        sd = sb("sd", [P, NT])
        rstd = sb("rstd", [P, NT])
        nmr = sb("nmr", [P, NT])
        dev = sb("dev", [P, NT])
        dev2 = sb("dev2", [P, NT])
        degn = sb("degn", [P, NT])
        dcol = sb("dcol", [P, 4])
        rsum = sb("rsum", [P, NT, H])
        z = sb("z", [P, UN, D])
        zT = sb("zT", [P, UN, D])
        kv_flat = kv[:, :, :, :].rearrange("p s c d -> p (s c d)")

        def row_buf(k, dt=F32):
            return kv_flat[0:NG, k * GE:(k + 1) * GE].bitcast(dt) if dt != F32 else kv_flat[0:NG, k * GE:(k + 1) * GE]

        src_i, dst_i, src_f, dst_f, tmp_f = row_buf(0, I32), row_buf(1, I32), row_buf(2), row_buf(3), row_buf(4)
        tmp_i = row_buf(5, I32)
        tmp_j = row_buf(6, I32)
        ext = sb("ext", [NG, 2])
        ext_i = sb("ext_i", [NG, 2], I32)
        ext_t = sb("ext_t", [NG, 2], I32)
        tiles = sb("tiles", [NG, 2])
        npair = sb("npair", [NG, 1])
        pair_f = prod[0:1, 0:3 * (NG + 2)].rearrange("a (k g) -> a k g", g=NG + 2)
        qf = q_parts[:, :, :].rearrange("p t d -> p (t d)")
        EC = NG * GC

        def carve(at, a, b):
            return qf[:, at:at + a * b].rearrange("p (a b) -> p a b", b=b)

        hot_lo = [carve(i * LO * HB, LO, HB) for i in range(2)]
        hot_hi = [carve(2 * LO * HB + i * HI * HB, HI, HB) for i in range(2)]
        AT = 2 * (LO + HI) * HB
        lo_ref = carve(AT, LO, HB)
        AT2 = AT + LO * HB
        qkv_flat = qkv[:, :, :].rearrange("p t d -> p (t d)")
        hi_ref = qkv_flat[:, 0:HI * HB // 2].bitcast(BF16).rearrange("p (a b) -> p a b", b=HB)
        src_lo = qkv_flat[:, 1000:1000 + EC // 2].bitcast(BF16)
        src_hi = qkv_flat[:, 1400:1400 + EC // 2].bitcast(BF16)
        src_ci = qkv_flat[:, 2000:2000 + EC].bitcast(I32)
        lo_i = qkv_flat[:, 3000:3000 + EC].bitcast(I32)
        hi_i = qkv_flat[:, 4000:4000 + EC].bitcast(I32)
        hid = kv_flat[:, 0:UN * FF].rearrange("p (u f) -> p u f", u=UN)

        ps = ctx.enter_context(nc.psum_tensor("ps", [P, 8, 512], F32))
        qd = [ps[:, 2 * b:2 * b + 2, :].rearrange("p b n -> p (b n)") for b in range(2)]
        agg = ps[:, 4:6, 0:MW]
        dst_rows = ps[:, 6:8, :].rearrange("p b n -> p (b n)")
        tp = [ps[:, 5 + u % 3, 0:P] for u in range(UN)]
        wide = [ps[:, u, :] for u in range(UN)]
        cnt = ps[0:LO, 4, 0:HI]

        kv_tab = [nc.dram_tensor(f"kv_tab{l}", [NT * P, 2 * D], F32) for l in range(L)]

        rows_clear = sem("rows_clear")
        consts = sem("consts")
        edges_in = sem("edges_in")
        x_clear = sem("x_clear")
        x_in = sem("x_in")
        raw_in = sems("raw_in")
        kept_in = sems("kept_in")
        chain = sem("chain")
        src_rows = sem("src_rows")
        src_T = sem("src_T")
        dst_T = sem("dst_T")
        cols_read = sem("cols_read")
        hot_ready = sem("hot_ready")
        hot_used = sem("hot_used")
        npair_ready = sem("npair_ready")
        pair_ps = sem("pair_ps")
        tab_ready = sem("tab_ready")
        sq_ready = sem("sq_ready")
        sq_sum = sem("sq_sum")
        deg_sd = sem("deg_sd")
        f_pos = sem("f_pos")
        f_posT_ps = sem("f_posT_ps")
        f_posT = sem("f_posT")
        f_cols = sem("f_cols")
        f_w_ps = sem("f_w_ps")
        f_w = sem("f_w")
        f_b_ps = sem("f_b_ps")
        f_done = sem("f_done")
        act_chain = sem("act_chain")
        st_done = sems("st_done", 2 * L + 1)
        mv_done = sem("mv_done")
        sd_done = sem("sd_done")
        rstd_done = sem("rstd_done")
        nmr_done = sem("nmr_done")
        z_done = sems("z_done", 2 * L)
        tp_done = sems("tp_done", 2 * L)
        zT_done = sems("zT_done", 2 * L)
        qkv_ps = sems("qkv_ps")
        qkv_deg = sems("qkv_deg")
        qkv_done = sems("qkv_done")
        tab_out = sems("tab_out")
        q_part = sems("q_part", 5)
        self_prod = sem("self_prod")
        self_dot = sem("self_dot")
        self_mask = sem("self_mask")
        self_att = sem("self_att")
        self_exp = sem("self_exp")
        self_msg = sem("self_msg")
        idx_ready = sems("idx_ready")
        kv_in = [sems(f"kv_in{l}_", SLOTS) for l in range(L)]
        row_ready = sems("row_ready")
        dist_done = sems("dist_done")
        hotT_ready = sems("hotT_ready")
        hotT_used = sems("hotT_used")
        prod_done = sems("prod_done")
        dot_done = sems("dot_done")
        mask_done = sems("mask_done")
        att_done = sems("att_done")
        exp_done = sems("exp_done")
        msg_done = sems("msg_done")
        gathering = sems("gathering")
        hot_done = sems("hot_done")
        agg_done = sems("agg_done")
        evac_done = sems("evac_done")
        rs_done = sem("rs_done")
        bo_added = sems("bo_added")
        b2_added = sems("b2_added")
        picked = sems("picked")
        ag_done = sems("ag_done")
        agT_ps = sems("agT_ps")
        agT_done = sems("agT_done")
        o_ps = sems("o_ps")
        x2_done = sems("x2_done")
        h_ps = sems("h_ps")
        h_done = sems("h_done")
        y_ps = sems("y_ps")
        y_b = sems("y_b")
        x3_done = sems("x3_done")
        first_in = sem("first_in")
        fin_add = sem("fin_add")
        fin_z = sem("fin_z")
        out_done = sem("out_done")

        block = ctx.enter_context(nc.Block())
        NCONST = 11
        RAW_LOADS = 16
        KEPT_LOADS = 4

        def pair_words(eng, base):
            read = {}

            def word(d):
                if d not in read:
                    w = eng.value_load(pair_tab[0:1, bass.ds(base + d + 2, 1)], min_val=0, max_val=MAXPAIRS * WORD + WORD - 1)
                    least = 0 if not isinstance(base, int) or base + d < 0 else 1
                    read[d] = (eng.snap((w >> WORD_BITS).with_bounds(min_val=least, max_val=MAXPAIRS)),
                               eng.snap((w & (WORD - 1)).with_bounds(min_val=1, max_val=MAXPAIRS + TOFF)))
                return read[d]
            return word

        def tile_of(eng, pr, shift):
            return eng.snap((pr + TOFF - shift).with_bounds(min_val=0, max_val=NT - 1))

        def after(eng, semaphore, n):
            if not isinstance(n, int) or n > 0:
                eng.wait_ge(semaphore, n)

        def pipelined(eng, *stages):
            def step(s, v):
                for lag, stage in stages:
                    if not isinstance(s, int) or 0 <= s - lag < NT:
                        stage(s - lag, (v - lag) % UN)

            peeled = 1 if all(lag == 0 for lag, _ in stages) else 2
            for s in range(peeled * UN):
                step(s, s % UN)
            with eng.Fori(peeled, NU) as i:
                for v in range(UN):
                    step(UN * i + v, v)
            for s in range(NT, NT + max(lag for lag, _ in stages)):
                step(s, s % UN)

        def at(t):
            return bass.ds(t, 1)

        @block.sync
        def _(sp):
            sp.wait_ge(rows_clear, 2)
            for rows, d in ((src_i, src_d), (dst_i, dst_d)):
                sp.dma_start(rows[0:NG - 1, :], d[0:(NG - 1) * GE].rearrange("(g e) -> g e", e=GE)).then_inc(edges_in, 16)
                sp.dma_start(rows[NG - 1:NG, 0:ELAST], d[(NG - 1) * GE:E].rearrange("(g e) -> g e", g=1)).then_inc(edges_in, 16)
            sp.dma_start(x[:, 0:NT - 1, :], x_d[0:(NT - 1) * P, :].rearrange("(t p) d -> p t d", p=P)).then_inc(x_in, 16)
            sp.wait_ge(x_clear, 1)
            sp.dma_start(x[0:NLAST, NT - 1, :], x_d[(NT - 1) * P:N, :]).then_inc(x_in, 16)
            for l in range(L):
                after(sp, f_done, l)

                def load(to, what, done=raw_in):
                    sp.dma_start(to, what).then_inc(done[l], 16)
                load(wpos, W["Wpos"][l])
                for n, k in enumerate(("Wq", "Wk", "Wv")):
                    load(wqkv[:, n * D:(n + 1) * D], W[k][l])
                for n, k in enumerate(("ln1_g", "ln1_b", "ln2_g", "ln2_b", "bpos", "bdeg")):
                    load(vecs[:, l, n:n + 1], W[k][l:l + 1, :].rearrange("a p -> p a"))
                load(vecs[:, l, 6:7], W["Wdeg"][l].rearrange("a p -> p a"))
                for n, k in enumerate(("bq", "bk", "bv")):
                    load(bqkv_row[:, n * D:(n + 1) * D], W[k][l:l + 1, :])
                load(w1, W["W1"][l])
                load(b1_row, W["b1"][l:l + 1, :])
            for l in range(L):
                load(wo[:, l, :], W["Wo"][l], kept_in)
                load(w2[:, l, :, :], W["W2"][l].rearrange("(c p) n -> p c n", p=P), kept_in)
                load(bo_bc[:, l, :], W["bo"][l, :].partition_broadcast(P), kept_in)
                load(b2_bc[:, l, :], W["b2"][l, :].partition_broadcast(P), kept_in)
            for l in range(L):
                table = kv_tab[l][:, :].rearrange("(t p) d -> p t d", p=P)
                with sp.Fori(0, NU) as i:
                    sp.wait_ge(qkv_done[l], UN * i + UN)
                    sp.dma_start(table[:, bass.ds(UN * i, UN), :], qkv[:, bass.ds(UN * i, UN), D:3 * D]).then_inc(tab_out[l], 16)
            sp.wait_ge(self_msg, L * NU)
            sp.wait_ge(q_part[4], L * NU)
            sp.wait_ge(tab_out[L - 1], 16 * NU)
            sp.dma_start(x_first[:, 0:NT - 1, :], x_d[0:(NT - 1) * P, :].rearrange("(t p) d -> p t d", p=P)).then_inc(first_in, 16)
            sp.dma_start(x_first[0:NLAST, NT - 1, :], x_d[(NT - 1) * P:N, :]).then_inc(first_in, 16)
            with sp.Fori(0, NU - 1) as i:
                sp.wait_ge(fin_z, UN * i + UN)
                sp.dma_start(out_d[bass.ds(UN * P * i, UN * P), :].rearrange("(t p) d -> p t d", p=P),
                             x[:, bass.ds(UN * i, UN), :]).then_inc(out_done, 16)
            sp.wait_ge(fin_z, NT)
            sp.dma_start(out_d[(NT - UN) * P:(NT - 1) * P, :].rearrange("(t p) d -> p t d", p=P),
                         x[:, NT - UN:NT - 1, :]).then_inc(out_done, 16)
            sp.dma_start(out_d[(NT - 1) * P:N, :], x[0:NLAST, NT - 1, :]).then_inc(out_done, 16)
            sp.wait_ge(out_done, 16 * (NU + 1))

        @block.gpsimd
        def _(pool):
            pool.memset(src_i, -1).then_inc(rows_clear, 1)
            pool.memset(dst_i, -1).then_inc(rows_clear, 1)
            pool.memset(x[:, NT - 1, :], 0.0).then_inc(x_clear, 1)
            pool.memset(ident[:, :], 0.0).then_inc(consts, 1)
            pool.wait_ge(consts, 1)
            pool.affine_select(out=ident[:, :], in_=ident[:, :], compare_op=ALU.not_equal, fill=1.0, base=0,
                               pattern=[[-1, P]], channel_multiplier=1).then_inc(consts, 1)
            pool.iota(lo_ref, pattern=[[1, LO], [0, HB]], base=0, channel_multiplier=0,
                      allow_small_or_imprecise_dtypes=True).then_inc(consts, 1)
            pool.iota(hi_ref, pattern=[[1, HI], [0, HB]], base=0, channel_multiplier=0,
                      allow_small_or_imprecise_dtypes=True).then_inc(consts, 1)
            pool.memset(ones[:, :], 1.0).then_inc(consts, 1)
            pool.memset(is_node[:, :], 1.0).then_inc(consts, 1)
            pool.memset(zeros[:, :], 0.0).then_inc(consts, 1)
            pool.wait_ge(consts, 7)
            pool.affine_select(out=is_node[:, :], in_=is_node[:, :], compare_op=ALU.is_ge, fill=0.0, base=N - 1,
                               pattern=[[-P, NT]], channel_multiplier=-1).then_inc(consts, 1)
            pool.affine_select(out=below[:, :], in_=ones[0:NG, 0:NG], compare_op=ALU.is_ge, fill=0.0, base=-1,
                               pattern=[[1, NG]], channel_multiplier=-1).then_inc(consts, 1)
            pool.iota(neg_node[:, :], pattern=[[-P, NT]], base=0, channel_multiplier=-1,
                      allow_small_or_imprecise_dtypes=True).then_inc(consts, 1)
            pool.iota(node_row[:, :], pattern=[[1, NT * P]], base=0, channel_multiplier=0,
                      allow_small_or_imprecise_dtypes=True).then_inc(consts, 1)

            for l in range(L):
                pool.wait_ge(raw_in[l], 16 * RAW_LOADS)
                nc.gpsimd.tensor_tensor(pos1, wpos, ident[:, :], ALU.add).then_inc(f_pos, 1)

            for l in range(L):
                pool.wait_ge(kept_in[l], 16 * KEPT_LOADS)
                with pool.Fori(0, NT) as t:
                    pool.wait_ge(z_done[2 * l], t + 1)
                    nc.gpsimd.tensor_tensor(x[:, at(t), :], x[:, at(t), :], bo_bc[:, l, :].unsqueeze(1), ALU.add).then_inc(bo_added[l], 1)
                pool.wait_ge(tab_out[l], 16 * NU)

                def gather(u, i, g, first=False):
                    pool.wait_ge(idx_ready[l], g + 1)
                    if not first:
                        pool.wait_ge(msg_done[l], g - SLOTS + 1)
                    pool.sem_inc(gathering[l], 1)
                    for c in range(GC):
                        pool.indirect_dma_start(kv[:, u, c, :], None, kv_tab[l][:, :],
                                                bass.IndirectOffsetOnAxis(ap=idx[:, u, c:c + 1], axis=0)).then_inc(kv_in[l][u], 16)

                for u in range(SLOTS):
                    gather(u, 0, u, first=True)
                with pool.Fori(1, NG // SLOTS) as i:
                    for u in range(SLOTS):
                        gather(u, i, SLOTS * i + u)
                for u in range(NG % SLOTS):
                    gather(u, NG // SLOTS, NG // SLOTS * SLOTS + u)
                with pool.Fori(0, NT) as t:
                    pool.wait_ge(z_done[2 * l + 1], t + 1)
                    nc.gpsimd.tensor_tensor(x[:, at(t), :], x[:, at(t), :], b2_bc[:, l, :].unsqueeze(1), ALU.add).then_inc(b2_added[l], 1)

        @block.scalar
        def _(act):
            links = [0]

            def link(ins):
                links[0] += 1
                ins.then_inc(act_chain, 1)
                act.wait_ge(act_chain, links[0])

            def stats_sd(k):
                act.wait_ge(mv_done, 3 * k + 3)
                nc.scalar.activation(sd[:, :], var[:, :], ACT.Sqrt, bias=eps_col[:, :]).then_inc(sd_done, 1)

            def normalise(k):
                def stage(t, u):
                    after(act, tp_done[k], t - UN + 1)
                    nc.scalar.activation(z[:, u:u + 1, :], x[:, at(t), :], ACT.Identity,
                                         bias=nmr[:, at(t)], scale=rstd[:, at(t)]).then_inc(z_done[k], 1)
                return stage

            for l in range(L):
                act.wait_ge(f_posT_ps, l + 1)
                nc.scalar.activation(posT, ps[:, 5, 0:P], ACT.Copy).then_inc(f_posT, 1)
                link(nc.scalar.activation(cvec[:, 0:1], ps[:, 5, P:P + 1], ACT.Identity, bias=vecs[:, l, 4:5]))
                link(nc.scalar.activation(cvec[:, 1:2], cvec[:, 0:1], ACT.Identity, bias=vecs[:, l, 5:6]))
                nc.scalar.activation(c_bc, ones[:, :], ACT.Copy, scale=cvec[:, 1:2])
                nc.scalar.activation(wd_bc, ones[:, :], ACT.Copy, scale=vecs[:, l, 6:7]).then_inc(f_cols, 1)
                act.wait_ge(f_w_ps, l + 1)
                nc.scalar.activation(wfold[:, l, :], ps[:, 6, 0:3 * D], ACT.Copy, scale=vecs[:, l, 0:1]).then_inc(f_w, 1)
                nc.scalar.activation(w1g[:, l, :], w1, ACT.Copy, scale=vecs[:, l, 2:3])
                act.wait_ge(f_b_ps, l + 1)
                nc.scalar.activation(bfold[:, l, :], ps[:, 7, 0:3 * D], ACT.Copy)
                nc.scalar.activation(degw[:, l, :], ps[:, 5, 0:3 * D], ACT.Copy)
                nc.scalar.activation(b1f[:, l, :], ps[:, 6, 0:FC], ACT.Copy).then_inc(f_done, 1)

            stats_sd(0)
            act.wait_ge(sq_sum, 1)
            nc.scalar.activation(dcol[:, 1:2], ps[:, 7, 0:1], ACT.Sqrt, scale=1.0 / (N - 1)).then_inc(deg_sd, 1)

            for l in range(L):
                if l:
                    stats_sd(2 * l)
                act.wait_ge(nmr_done, 2 * l + 1)

                def copy_zT(t, u):
                    act.wait_ge(tp_done[2 * l], t + 1)
                    after(act, qkv_ps[l], t - UN + 1)
                    nc.scalar.activation(zT[:, u, :], tp[u], ACT.Copy).then_inc(zT_done[2 * l], 1)
                pipelined(act, (0, normalise(2 * l)), (1, copy_zT))
                with act.Fori(0, NU) as i:
                    block_ = bass.ds(UN * i, UN)
                    act.wait_ge(qkv_done[l], UN * i + UN)
                    nc.scalar.activation(q_parts[:, block_, 0:D], qkv[:, block_, 0:D], ACT.Copy).then_inc(q_part[0], 1)
                with act.Fori(0, NU) as i:
                    act.wait_ge(self_att, l * NU + i + 1)
                    nc.scalar.activation(acc[:, bass.ds(UN * i, UN), D:MW],
                                         att[:, 0:UN * H].rearrange("p (t h) -> p t h", h=H), ACT.Exp,
                                         scale=1.0 / SCALE).then_inc(self_exp, 1)
                act.sem_inc(hotT_used[l], 2)
                act.sem_inc(hotT_ready[l], 1)
                if l == 0:
                    act.wait_ge(tab_ready, 1)

                def pick_rows(g):
                    nc.scalar.activation(pick[:, bass.ds(g % 2, 1), :], spread(ident[0:NG, at(g)], 2, P), ACT.Copy).then_inc(picked[l], 1)

                def one_hots(word, d, g):
                    a = word(d - 1)[0]
                    b, shift = word(d)
                    act.wait_ge(row_ready[l], g + 1)
                    pick_rows(g + 2)
                    with act.Fori(a, b) as pr:
                        t = tile_of(act, pr, shift)
                        act.wait_ge(hotT_ready[l], pr + 1)
                        nc.scalar.activation(dist[:, :], dst_rows, ACT.Abs, bias=neg_node[:, at(t)]).then_inc(dist_done[l], 1)
                        act.wait_ge(dist_done[l], pr + 1)
                        act.wait_ge(hotT_used[l], pr + 1)
                        nc.scalar.activation(hotT[:, bass.ds(pr % 2, 1), :], dist[:, :], ACT.Relu, bias=1.0, scale=-1.0).then_inc(hotT_ready[l], 1)

                def weights(u, g):
                    act.wait_ge(att_done[l], g + 1)
                    nc.scalar.activation(msg[:, u % 2, :, D:MW], att[:, :].rearrange("p (c h) -> p c h", h=H), ACT.Exp,
                                         scale=1.0 / SCALE).then_inc(exp_done[l], 1)

                pick_rows(0)
                pick_rows(1)
                word = pair_words(act, 0)
                one_hots(word, 0, 0)
                one_hots(word, 1, 1)
                with act.Fori(0, NG // SLOTS) as i:
                    word = pair_words(act, SLOTS * i)
                    for u in range(SLOTS):
                        weights(u, SLOTS * i + u)
                        one_hots(word, u + 2, SLOTS * i + u + 2)
                weights(0, NG - 2)
                weights(1, NG - 1)
                def copy_agT(t, u):
                    act.wait_ge(agT_ps[l], t + 1)
                    after(act, o_ps[l], t - UN + 1)
                    nc.scalar.activation(zT[:, u, :], tp[u], ACT.Copy).then_inc(agT_done[l], 1)
                pipelined(act, (0, copy_agT))
                stats_sd(2 * l + 1)
                act.wait_ge(nmr_done, 2 * l + 1 + 1)

                def gelu(t, u):
                    act.wait_ge(h_ps[l], t + 1)
                    after(act, y_ps[l], t - UN + 1)
                    for c in range(FC):
                        last = nc.scalar.activation(hid[:, u, c * P:(c + 1) * P], wide[u][:, c * P:(c + 1) * P], ACT.Gelu,
                                                    bias=b1f[:, l, c:c + 1])
                    last.then_inc(h_done[l], 1)
                pipelined(act, (0, normalise(2 * l + 1)), (2, gelu))
            stats_sd(2 * L)
            act.wait_ge(nmr_done, 2 * L + 1)
            with act.Fori(0, NT) as t:
                nc.scalar.activation(x[:, bass.ds(t, 1), :], x[:, bass.ds(t, 1), :], ACT.Identity,
                                     bias=nmr[:, bass.ds(t, 1)], scale=rstd[:, bass.ds(t, 1)]).then_inc(fin_z, 1)

        @block.vector
        def _(dve):
            links = [0]

            def link(ins):
                links[0] += 1
                ins.then_inc(chain, 1)
                dve.wait_ge(chain, links[0])

            def tile_stats(k, t):
                nc.vector.bn_stats(stats[:, at(t), :], x[:, at(t), :]).then_inc(st_done[k], 1)

            def variance(k):
                dve.wait_ge(st_done[k], NT)
                nc.vector.tensor_tensor(half_gap[:, :], stats[:, :, 1], stats[:, :, 4], ALU.subtract)
                nc.vector.tensor_tensor(mean2[:, :], stats[:, :, 1], stats[:, :, 4], ALU.add)
                nc.vector.tensor_tensor(sq_dev[:, :], stats[:, :, 2], stats[:, :, 5], ALU.add).then_inc(mv_done, 1)
                dve.wait_ge(mv_done, 3 * k + 1)
                nc.vector.scalar_tensor_tensor(out=gap2[:, :], in0=half_gap[:, :], scalar=0.25, in1=half_gap[:, :],
                                               op0=ALU.mult, op1=ALU.mult).then_inc(mv_done, 1)
                dve.wait_ge(mv_done, 3 * k + 2)
                nc.vector.scalar_tensor_tensor(out=var[:, :], in0=sq_dev[:, :], scalar=1.0 / D, in1=gap2[:, :],
                                               op0=ALU.mult, op1=ALU.add).then_inc(mv_done, 1)

            def scales(k):
                dve.wait_ge(sd_done, k + 1)
                nc.vector.reciprocal(rstd[:, :], sd[:, :]).then_inc(rstd_done, 1)
                dve.wait_ge(rstd_done, k + 1)
                nc.vector.scalar_tensor_tensor(out=nmr[:, :], in0=mean2[:, :], scalar=-0.5, in1=rstd[:, :],
                                               op0=ALU.mult, op1=ALU.mult).then_inc(nmr_done, 1)

            link(nc.vector.memset(eps_col[:, :], EPS))
            link(nc.vector.memset(dev[:, :], 0.0))
            dve.wait_ge(edges_in, 64)
            nc.vector.tensor_copy(src_f, src_i).then_inc(src_rows, 1)
            nc.vector.tensor_copy(dst_f, dst_i).then_inc(src_rows, 1)
            dve.wait_ge(x_in, 32)
            with dve.Fori(0, NT) as t:
                tile_stats(0, t)
            variance(0)
            def cols(bank):
                return ps[:, bank:bank + 2, 0:4 * NG]
            dve.wait_ge(src_T, 1)
            link(nc.vector.tensor_copy(src_ci.rearrange("p (b n) -> p b n", b=2), cols(0)))
            link(nc.vector.tensor_single_scalar(lo_i, src_ci, LO - 1, ALU.bitwise_and))
            link(nc.vector.tensor_single_scalar(hi_i, src_ci, LO.bit_length() - 1, ALU.arith_shift_right))
            link(nc.vector.tensor_copy(src_lo, lo_i))
            link(nc.vector.tensor_copy(src_hi, hi_i))
            dve.wait_ge(consts, 4)
            with dve.Fori(0, NHB // 2) as i:
                for b in range(2):
                    k = 2 * i + b
                    dve.wait_ge(hot_used, k + 1)
                    nc.vector.tensor_tensor(hot_lo[b], lo_ref, spread(src_lo[:, bass.ds(k * HB, HB)], 1, LO), ALU.is_equal)
                    nc.vector.tensor_tensor(hot_hi[b], hi_ref, spread(src_hi[:, bass.ds(k * HB, HB)], 1, HI), ALU.is_equal).then_inc(hot_ready, 1)
            dve.wait_ge(hot_used, NHB + 2)
            dve.wait_ge(consts, NCONST)
            link(nc.vector.tensor_copy(dev[0:LO, 0:NT], cnt[:, 0:HI:2]))
            link(nc.vector.tensor_copy(dev[LO:2 * LO, 0:HI // 2], cnt[:, 1:HI:2]))
            link(nc.vector.scalar_tensor_tensor(out=dev[:, :], in0=dev[:, :], scalar=1.0 - MEAN_DEG, in1=is_node[:, :],
                                                op0=ALU.add, op1=ALU.mult))
            link(nc.vector.tensor_tensor(dev2[:, :], dev[:, :], dev[:, :], ALU.mult))
            nc.vector.tensor_reduce(dcol[:, 0:1], dev2[:, :], AX.X, ALU.add).then_inc(sq_ready, 1)
            dve.wait_ge(dst_T, 1)
            nc.vector.tensor_copy(dst_col[:, :, :].rearrange("p (b c) g -> p b (c g)", b=2), cols(2)).then_inc(cols_read, 1)
            nc.vector.tensor_scalar(src_idx[:, :, :].rearrange("p (b c) g -> p b (c g)", b=2), cols(0), 0.0, None, ALU.max).then_inc(cols_read, 1)
            dve.wait_ge(deg_sd, 1)
            link(nc.vector.tensor_scalar(dcol[:, 2:3], dcol[:, 1:2], 1e-6, None, ALU.add))
            link(nc.vector.reciprocal(dcol[:, 3:4], dcol[:, 2:3]))
            link(nc.vector.tensor_scalar(degn[:, :], dev[:, :], dcol[:, 3:4], None, ALU.mult))

            def edge_tables():
                dve.wait_ge(src_rows, 2)
                link(nc.vector.tensor_single_scalar(tmp_i, dst_i, 7, ALU.arith_shift_right))
                link(nc.vector.tensor_single_scalar(tmp_j, dst_i, P - 1, ALU.bitwise_and))
                link(nc.vector.tensor_scalar(dst_hi[:, :], tmp_i, float(P), None, ALU.mult))
                link(nc.vector.tensor_copy(dst_lo[:, :], tmp_j))
                link(nc.vector.tensor_scalar(tmp_f, dst_f, 0.0, float(2 * NT * P), ALU.is_lt, ALU.mult))
                link(nc.vector.tensor_tensor(tmp_f, tmp_f, dst_f, ALU.add))
                link(nc.vector.tensor_reduce(ext[:, 0:1], tmp_f, AX.X, ALU.min))
                link(nc.vector.tensor_reduce(ext[:, 1:2], dst_f, AX.X, ALU.max))
                link(nc.vector.tensor_copy(ext_i[:, :], ext[:, :]))
                link(nc.vector.tensor_single_scalar(ext_t[:, :], ext_i[:, :], 7, ALU.arith_shift_right))
                link(nc.vector.tensor_copy(tiles[:, :], ext_t[:, :]))
                nc.vector.scalar_tensor_tensor(out=npair[:, :], in0=tiles[:, 1:2], scalar=1.0, in1=tiles[:, 0:1],
                                               op0=ALU.add, op1=ALU.subtract).then_inc(npair_ready, 1)
                dve.wait_ge(pair_ps, 1)
                first_ps, count_ps, tile_ps = (ps[0:1, 7, 128 * k:128 * k + NG] for k in (1, 2, 3))
                link(nc.vector.memset(pair_f[:, 2, :], float(TOFF - 1)))
                link(nc.vector.tensor_copy(pair_f[:, 0, 2:], first_ps))
                link(nc.vector.tensor_tensor(pair_f[:, 1, 2:], pair_f[:, 0, 2:], count_ps, ALU.add))
                link(nc.vector.scalar_tensor_tensor(out=pair_f[:, 0, 2:], in0=pair_f[:, 0, 2:], scalar=float(TOFF), in1=tile_ps,
                                                    op0=ALU.add, op1=ALU.subtract))
                link(nc.vector.scalar_tensor_tensor(out=pair_f[:, 2, 2:], in0=pair_f[:, 1, 2:], scalar=float(WORD), in1=pair_f[:, 0, 2:],
                                                    op0=ALU.mult, op1=ALU.add))
                nc.vector.tensor_copy(pair_tab[:, :], pair_f[:, 2, :]).then_inc(tab_ready, 1)
                dve.wait_ge(tab_ready, 1)

            for l in range(L):
                scales(2 * l)
                if l == 0:
                    dve.wait_ge(f_done, L)

                def add_degree(t, u):
                    dve.wait_ge(qkv_ps[l], t + 1)
                    nc.vector.scalar_tensor_tensor(out=qkv[:, at(t), :], in0=degw[:, l, :].unsqueeze(1), scalar=degn[:, at(t)],
                                                   in1=wide[u][:, 0:3 * D].unsqueeze(1), op0=ALU.mult, op1=ALU.add).then_inc(qkv_deg[l], 1)

                def add_bias(t, u):
                    dve.wait_ge(qkv_deg[l], t + 1)
                    nc.vector.tensor_tensor(qkv[:, at(t), :], qkv[:, at(t), :], bfold[:, l, :].unsqueeze(1), ALU.add).then_inc(qkv_done[l], 1)
                pipelined(dve, (0, add_degree), (1, add_bias))
                if l == 0:
                    edge_tables()

                def fetch_idx(u, g):
                    nc.vector.tensor_copy(idx[:, u, :], src_idx[:, :, bass.ds(g, 1)].rearrange("p c o -> p (c o)")).then_inc(idx_ready[l], 1)
                if l == 0:
                    dve.wait_ge(cols_read, 2)
                for u in range(SLOTS):
                    fetch_idx(u, u)

                with dve.Fori(0, NU) as i:
                    tb = bass.ds(UN * i, UN)
                    rest = prod[:, 0:UN * D].rearrange("p (t d) -> p t d", d=D)
                    dve.wait_ge(qkv_done[l], UN * i + UN)
                    dve.wait_ge(q_part[0], l * NU + i + 1)
                    nc.vector.tensor_tensor(rest, qkv[:, tb, 0:D], q_parts[:, tb, 0:D], ALU.subtract).then_inc(q_part[1], 1)
                    dve.wait_ge(q_part[1], l * NU + i + 1)
                    nc.vector.tensor_copy(q_parts[:, tb, D:2 * D], rest).then_inc(q_part[2], 1)
                    dve.wait_ge(q_part[2], l * NU + i + 1)
                    nc.vector.tensor_tensor(rest, rest, q_parts[:, tb, D:2 * D], ALU.subtract).then_inc(q_part[3], 1)
                    dve.wait_ge(q_part[3], l * NU + i + 1)
                    nc.vector.tensor_copy(q_parts[:, tb, 2 * D:3 * D], rest).then_inc(q_part[4], 1)
                    dve.wait_ge(q_part[4], l * NU + i + 1)
                    n = UN * H
                    nc.vector.tensor_tensor(rest, qkv[:, tb, 0:D], qkv[:, tb, D:2 * D], ALU.mult).then_inc(self_prod, 1)
                    dve.wait_ge(self_prod, l * NU + i + 1)
                    nc.vector.tensor_reduce(dots[:, 0:n], prod[:, 0:UN * D].rearrange("p (n d) -> p n d", d=HD), AX.X, ALU.add).then_inc(self_dot, 1)
                    dve.wait_ge(self_dot, l * NU + i + 1)
                    nc.vector.tensor_tensor(not_nan[:, 0:n], dots[:, 0:n], dots[:, 0:n], ALU.is_equal)
                    nc.vector.tensor_scalar(clipped[:, 0:n], dots[:, 0:n], CLIP * SCALE, -CLIP * SCALE, ALU.min, ALU.max).then_inc(self_mask, 1)
                    dve.wait_ge(self_mask, l * NU + i + 1)
                    nc.vector.tensor_tensor(att[:, 0:n], clipped[:, 0:n], not_nan[:, 0:n], ALU.mult).then_inc(self_att, 1)
                    dve.wait_ge(self_exp, l * NU + i + 1)
                    nc.vector.tensor_tensor(acc[:, tb, 0:D].rearrange("p t (h d) -> p t h d", d=HD),
                                            qkv[:, tb, 2 * D:3 * D].rearrange("p t (h d) -> p t h d", d=HD),
                                            spread(acc[:, tb, D:MW], 3, HD), ALU.mult).then_inc(self_msg, 1)
                dve.wait_ge(self_msg, l * NU + NU)

                nc.vector.memset(agg[:, 1, :], 0.0).then_inc(agg_done[l], 1)
                dve.sem_inc(evac_done[l], 1)

                def evacuate(pr_plus_1, shift):
                    t = tile_of(dve, pr_plus_1 - 2, shift)
                    dve.wait_ge(agg_done[l], pr_plus_1)
                    dve.wait_ge(evac_done[l], pr_plus_1)
                    nc.vector.tensor_tensor(acc[:, at(t), :], acc[:, at(t), :],
                                            agg[:, bass.ds(pr_plus_1 % 2, 1), :], ALU.add).then_inc(evac_done[l], 1)

                def one_hot(u, g, t):
                    nc.vector.tensor_tensor(hot[:, u % 2, :, :], spread(node_row[:, bass.ds(t * P, P)], 1, GC),
                                            dst_col[:, :, at(g)].broadcast_to([P, GC, P]), ALU.is_equal).then_inc(hot_done[l], 1)

                def further_tiles(u, g, a, b, shift):
                    with dve.If(b > a + 1):
                        with dve.Fori(a + 1, b) as pr:
                            dve.wait_ge(agg_done[l], pr + 1)
                            one_hot(u, g, tile_of(dve, pr, shift))
                            evacuate(pr + 1, shift)

                def edge_group(u, i, g, word, d, fetch=True, ahead=True):
                    half = msg[:, u % 2, :, :]
                    b, shift = word(d)
                    dve.wait_ge(kv_in[l][u], 16 * GC * (i + 1))
                    dve.wait_ge(hotT_used[l], b + 2)
                    nc.vector.tensor_tensor(prod[:, :].rearrange("p (c d) -> p c d", d=D), kv[:, u, :, 0:D],
                                            qd[u % 2].rearrange("p (c d) -> p c d", d=D), ALU.mult).then_inc(prod_done[l], 1)
                    if fetch:
                        fetch_idx(u, g + SLOTS)
                    dve.wait_ge(prod_done[l], g + 1)
                    nc.vector.tensor_reduce(dots[:, :], prod[:, :].rearrange("p (n d) -> p n d", d=HD), AX.X, ALU.add).then_inc(dot_done[l], 1)
                    dve.wait_ge(dot_done[l], g + 1)
                    nc.vector.tensor_tensor(not_nan[:, :], dots[:, :], dots[:, :], ALU.is_equal)
                    nc.vector.tensor_scalar(clipped[:, :], dots[:, :], CLIP * SCALE, -CLIP * SCALE, ALU.min, ALU.max).then_inc(mask_done[l], 1)
                    dve.wait_ge(mask_done[l], g + 1)
                    nc.vector.tensor_tensor(att[:, :], clipped[:, :], not_nan[:, :], ALU.mult).then_inc(att_done[l], 1)
                    a, last_shift = word(d - 1)
                    before = g - 1 if isinstance(g, int) else (g - 1).with_bounds(min_val=0, max_val=NG - 1)
                    further_tiles(u + 1, before, word(d - 2)[0], a, last_shift)
                    one_hot(u, g, tile_of(dve, a, shift))
                    if ahead:
                        word(d + 1)
                    dve.wait_ge(exp_done[l], g + 1)
                    nc.vector.tensor_tensor(half[:, :, 0:D].rearrange("p c (h d) -> p c h d", d=HD),
                                            kv[:, u, :, D:2 * D].rearrange("p c (h d) -> p c h d", d=HD),
                                            spread(half[:, :, D:MW], 3, HD), ALU.mult).then_inc(msg_done[l], 1)
                    evacuate(a + 1, last_shift)

                with dve.Fori(0, NG // SLOTS - 1) as i:
                    word = pair_words(dve, SLOTS * i)
                    for u in range(SLOTS):
                        edge_group(u, i, SLOTS * i + u, word, u, ahead=u < SLOTS - 1)
                word = pair_words(dve, 0)
                for g in range((NG // SLOTS - 1) * SLOTS, NG):
                    edge_group(g % SLOTS, g // SLOTS, g, word, g, fetch=g + SLOTS < NG, ahead=g < NG - 1)
                end, shift = word(NG - 1)
                further_tiles(NG - 1, NG - 1, word(NG - 2)[0], end, shift)
                evacuate(end + 1, shift)
                dve.wait_ge(evac_done[l], end + 2)

                nc.vector.reciprocal(rsum[:, :, :], acc[:, :, D:MW]).then_inc(rs_done, 1)
                dve.wait_ge(rs_done, l + 1)
                dve.wait_ge(bo_added[l], NT)

                def quotient(t, u):
                    after(dve, agT_ps[l], t - UN + 1)
                    nc.vector.tensor_tensor(z[:, u, :].rearrange("p (h d) -> p h d", d=HD).unsqueeze(1),
                                            acc[:, at(t), 0:D].rearrange("p t (h d) -> p t h d", d=HD),
                                            spread(rsum[:, at(t), :], 3, HD), ALU.mult).then_inc(ag_done[l], 1)

                def residual(t, u):
                    dve.wait_ge(o_ps[l], t + 1)
                    nc.vector.tensor_tensor(x[:, at(t), :], x[:, at(t), :], wide[u][:, 0:D].unsqueeze(1), ALU.add).then_inc(x2_done[l], 1)

                def stats_2(t, u):
                    dve.wait_ge(x2_done[l], t + 1)
                    tile_stats(2 * l + 1, t)
                pipelined(dve, (0, quotient), (2, residual), (3, stats_2))
                variance(2 * l + 1)
                scales(2 * l + 1)

                def copy_zT(t, u):
                    dve.wait_ge(tp_done[2 * l + 1], t + 1)
                    after(dve, h_ps[l], t - UN + 1)
                    nc.vector.tensor_copy(zT[:, u, :], tp[u]).then_inc(zT_done[2 * l + 1], 1)

                def residual_2(t, u):
                    dve.wait_ge(b2_added[l], t + 1)
                    dve.wait_ge(y_ps[l], t + 1)
                    nc.vector.tensor_tensor(x[:, at(t), :], x[:, at(t), :], wide[u][:, 0:D].unsqueeze(1), ALU.add).then_inc(x3_done[l], 1)

                def residual_first(t, u):
                    dve.wait_ge(x3_done[l], t + 1)
                    nc.vector.tensor_tensor(x[:, at(t), :], x[:, at(t), :], x_first[:, at(t), :], ALU.add).then_inc(fin_add, 1)

                def stats_3(t, u):
                    if l == L - 1:
                        dve.wait_ge(fin_add, t + 1)
                    else:
                        dve.wait_ge(x3_done[l], t + 1)
                    tile_stats(2 * l + 2, t)
                if l == L - 1:
                    dve.wait_ge(first_in, 32)
                    pipelined(dve, (0, copy_zT), (3, residual_2), (4, residual_first), (5, stats_3))
                else:
                    pipelined(dve, (0, copy_zT), (3, residual_2), (4, stats_3))
                variance(2 * l + 2)
            scales(2 * L)

        @block.tensor
        def _(pe):
            MM = nc.tensor.matmul
            pe.sem_inc(hot_used, 2)
            pe.wait_ge(consts, 2)
            pe.wait_ge(src_rows, 2)
            for which, bank, done in ((src_f, 0, src_T), (dst_f, 2, dst_T)):
                for c in range(GC):
                    last = nc.tensor.transpose(ps[:, bank + c // 4, (c % 4) * NG:(c % 4 + 1) * NG], which[:, c * P:(c + 1) * P], ident[0:NG, 0:NG])
                last.then_inc(done, 1)
            def count(i):
                for b in range(2):
                    pe.wait_ge(hot_ready, 2 * i + b + 1)
                    for c in range(HB):
                        last = MM(cnt, hot_lo[b][:, :, c], hot_hi[b][:, :, c], start=False, stop=True, skip_group_check=True)
                    last.then_inc(hot_used, 1)

            def fold_transpose(l):
                pe.wait_ge(f_pos, l + 1)
                after(pe, f_done, l)
                nc.tensor.transpose(ps[:, 5, 0:P], pos1, ident[:, :])
                MM(ps[:, 5, P:P + 1], pos1, vecs[:, l, 1:2], start=True, stop=True).then_inc(f_posT_ps, 1)

            def fold_weights(l):
                pe.wait_ge(f_posT, l + 1)
                MM(ps[:, 6, 0:3 * D], posT, wqkv, start=True, stop=True).then_inc(f_w_ps, 1)

            def fold_biases(l):
                pe.wait_ge(f_cols, l + 1)
                MM(ps[:, 7, 0:3 * D], c_bc, wqkv, start=True, stop=False)
                MM(ps[:, 7, 0:3 * D], ones[0:1, :], bqkv_row, start=False, stop=True)
                MM(ps[:, 5, 0:3 * D], wd_bc, wqkv, start=True, stop=True)
                pe.wait_ge(f_w, l + 1)
                for c in range(FC):
                    MM(ps[:, 6, c:c + 1], w1[:, c * P:(c + 1) * P], vecs[:, l, 3:4], start=True, stop=False)
                    last = MM(ps[:, 6, c:c + 1], b1_row[:, c * P:(c + 1) * P], ones[0:1, 0:1], start=False, stop=True)
                last.then_inc(f_b_ps, 1)

            pe.wait_ge(consts, 7)
            MM(cnt, zeros[:, 0:LO], zeros[:, 0:HI], start=True, stop=False, skip_group_check=True)
            with pe.Fori(0, FOLD_AT) as i:
                count(i)
            for k, (fold, l) in enumerate((f, l) for l in range(L) for f in (fold_transpose, fold_weights, fold_biases)):
                fold(l)
                count(FOLD_AT + k)
            with pe.Fori(FOLD_AT + 3 * L, NHB // 2) as i:
                count(i)
            pe.wait_ge(sq_ready, 1)
            pe.wait_ge(f_done, L)
            MM(ps[:, 7, 0:1], ones[:, :], dcol[:, 0:1], start=True, stop=True).then_inc(sq_sum, 1)

            def pair_numbers():
                pe.wait_ge(npair_ready, 1)
                MM(ps[0:1, 7, 128:128 + NG], npair[:, :], below[:, :], start=True, stop=True)
                MM(ps[0:1, 7, 256:256 + NG], npair[:, :], ident[0:NG, 0:NG], start=True, stop=True)
                MM(ps[0:1, 7, 384:384 + NG], tiles[:, 0:1], ident[0:NG, 0:NG], start=True, stop=True).then_inc(pair_ps, 1)

            for l in range(L):
                def transposed(k):
                    def stage(t, u):
                        pe.wait_ge(z_done[k], t + 1)
                        after(pe, zT_done[k], t - 1)
                        nc.tensor.transpose(tp[u], z[:, u, :], ident[:, :]).then_inc(tp_done[k], 1)
                    return stage

                def project_qkv(t, u):
                    pe.wait_ge(zT_done[2 * l], t + 1)
                    after(pe, qkv_deg[l], t - UN + 1)
                    MM(wide[u][:, 0:3 * D], zT[:, u, :], wfold[:, l, :], start=True, stop=True).then_inc(qkv_ps[l], 1)
                if l == 0:
                    pe.wait_ge(cols_read, 2)
                pipelined(pe, (0, transposed(2 * l)), (1, project_qkv))
                if l == 0:
                    pair_numbers()

                if l == 0:
                    pe.wait_ge(tab_ready, 1)
                pe.wait_ge(qkv_done[l], NT)
                pe.wait_ge(q_part[4], l * NU + NU)

                def broadcast_rows(gp, g, a):
                    pe.wait_ge(picked[l], g + 1)
                    if a is not None:
                        pe.wait_ge(dist_done[l], a)
                    for half in range(2):
                        cut = slice(512 * half, 512 * half + 512)
                        for part, start in ((dst_hi, True), (dst_lo, False)):
                            last = MM(dst_rows[:, cut], pick[:, gp, :], part[:, cut], start=start, stop=not start)
                    last.then_inc(row_ready[l], 1)

                def gather_q(u, g, a, b, shift):
                    if not (isinstance(g, int) and g < 2):
                        pe.wait_ge(prod_done[l], g - 1)
                    def gather_pair(pr, first):
                        t = tile_of(pe, pr, shift)
                        pe.wait_ge(hotT_ready[l], pr + 2)
                        for c in range(GC):
                            for k in range(3):
                                last = MM(qd[u % 2][:, c * P:(c + 1) * P], hotT[:, bass.ds(pr % 2, 1), c * P:(c + 1) * P],
                                          q_parts[:, at(t), k * D:(k + 1) * D], start=first and c % 4 == 0 and k == 0,
                                          stop=True, skip_group_check=True)
                        last.then_inc(hotT_used[l], 1)
                    gather_pair(a, True)
                    with pe.If(b > a + 1):
                        with pe.Fori(a + 1, b) as pr:
                            gather_pair(pr, False)

                def sum_pair(u, pr):
                    pe.wait_ge(hot_done[l], pr + 1)
                    pe.wait_ge(evac_done[l], pr + 1)
                    for c in range(GC):
                        last = MM(agg[:, bass.ds(pr % 2, 1), :], hot[:, u % 2, c, :], msg[:, u % 2, c, :], start=(c == 0), stop=(c == GC - 1))
                    last.then_inc(agg_done[l], 1)

                def sum_further(u, a, b):
                    with pe.If(b > a + 1):
                        with pe.Fori(a + 1, b) as pr:
                            sum_pair(u, pr)

                def pe_group(u, g, word, d, more=True, ahead=True):
                    if more:
                        gather_q(u + 1, g + 1, word(d)[0], *word(d + 1))
                    sum_further(u + 1, word(d - 2)[0], word(d - 1)[0])
                    if ahead:
                        broadcast_rows(u % 2, g + 2, word(d + 1)[0])
                    pe.wait_ge(msg_done[l], g + 1)
                    sum_pair(u, word(d - 1)[0])

                word = pair_words(pe, 0)
                broadcast_rows(0, 0, None)
                gather_q(0, 0, word(-1)[0], *word(0))
                broadcast_rows(1, 1, word(0)[0])
                for g in range(SLOTS):
                    pe_group(g, g, word, g)
                with pe.Fori(1, NG // SLOTS) as i:
                    word = pair_words(pe, SLOTS * i)
                    for u in range(SLOTS):
                        pe_group(u, SLOTS * i + u, word, u)
                word = pair_words(pe, 0)
                pe_group(0, NG - 2, word, NG - 2, ahead=False)
                pe_group(1, NG - 1, word, NG - 1, more=False, ahead=False)
                sum_further(1, word(NG - 2)[0], word(NG - 1)[0])

                def transpose_ag(t, u):
                    pe.wait_ge(ag_done[l], t + 1)
                    after(pe, agT_done[l], t - 1)
                    nc.tensor.transpose(tp[u], z[:, u, :], ident[:, :]).then_inc(agT_ps[l], 1)

                def project_out(t, u):
                    pe.wait_ge(agT_done[l], t + 1)
                    after(pe, x2_done[l], t - UN + 1)
                    MM(wide[u][:, 0:D], zT[:, u, :], wo[:, l, :], start=True, stop=True).then_inc(o_ps[l], 1)
                pipelined(pe, (0, transpose_ag), (1, project_out))

                def hidden(t, u):
                    pe.wait_ge(zT_done[2 * l + 1], t + 1)
                    after(pe, x3_done[l], t - UN + 1)
                    for c in range(FC):
                        last = MM(wide[u][:, c * P:(c + 1) * P], w1g[:, l, c * P:(c + 1) * P], zT[:, u, :], start=True, stop=True)
                    last.then_inc(h_ps[l], 1)

                def project_ffn(t, u):
                    pe.wait_ge(h_done[l], t + 1)
                    for c in range(FC):
                        last = MM(wide[u][:, 0:D], hid[:, u, c * P:(c + 1) * P], w2[:, l, c, :], start=(c == 0), stop=(c == FC - 1))
                    last.then_inc(y_ps[l], 1)
                pipelined(pe, (0, transposed(2 * l + 1)), (1, hidden), (3, project_ffn))


_WEIGHTS = ["Wq", "bq", "Wk", "bk", "Wv", "bv", "Wo", "bo", "Wpos", "bpos", "Wdeg", "bdeg",
            "ln1_g", "ln1_b", "ln2_g", "ln2_b", "W1", "b1", "W2", "b2"]


def kernel(**inputs):
    import numpy as _np
    import concourse.bacc as _bacc
    from concourse import mybir as _mybir
    from concourse.bass_utils import run_bass_kernel_spmd as _run

    nc = _bacc.Bacc("TRN2", target_bir_lowering=False, num_devices=1)
    arrays = {}

    def given(name):
        a = _np.ascontiguousarray(inputs[name])
        arrays[f"in_{name}"] = a
        return nc.dram_tensor(f"in_{name}", a.shape, _mybir.dt.from_np(a.dtype), kind="ExternalInput").ap()

    x, src, dst = given("x"), given("src"), given("dst")
    weights = {k: given(f"L0_gnn_{k}") for k in _WEIGHTS}
    out = nc.dram_tensor("out_0", (N, D), _mybir.dt.float32, kind="ExternalOutput").ap()
    gnn_program(nc, x, src, dst, weights, out)
    r = _run(nc, [arrays], core_ids=[0])
    return r.results[0]["out_0"]
```

```python
import numpy as np
import concourse.bass as bass
from concourse import mybir
from contextlib import ExitStack

F32 = mybir.dt.float32
BF16 = mybir.dt.bfloat16
I32 = mybir.dt.int32
ALU = mybir.AluOpType
ACT = mybir.ActivationFunctionType
AX = mybir.AxisListType

N, E, D, H, L, FF = 3125, 100000, 128, 8, 2, 512
HD = D // H
P = 128
NT = -(-N // P)
NLAST = N - (NT - 1) * P
GC = 8
GE = GC * P
NG = -(-E // GE)
ELAST = E - (NG - 1) * GE
LAST_CHUNKS = -(-ELAST // P)
MW = D + H
SLOTS = 4
UN = 5
NU = NT // UN
FC = FF // P
LO = 64
HI = -(-N // LO)
HB = 28
NHB = NG * GC // HB
FOLD_AT = 3
CLOSING_ACT = 2
RESIDUAL_AT = {2: 3, 4: 2}
EPS = 1e-5
CLIP = 50.0
SCALE = float(HD) ** 0.5
MEAN_DEG = (E + N) / N
TOFF = 32
MAXPAIRS = NG * NT
WORD_BITS = 12
WORD = 1 << WORD_BITS
assert MAXPAIRS + TOFF < WORD and MAXPAIRS * WORD < 1 << 24
assert NT % UN == 0 and NHB * HB == NG * GC and NHB % 2 == 0 and NG % SLOTS == 2
assert NG // SLOTS - 2 < NT < NG // SLOTS + 2


def gnn_program(nc, x_d, src_d, dst_d, W, out_d):
    ctx = ExitStack()
    with ctx:
        def sb(name, shape, dt=F32):
            return ctx.enter_context(nc.sbuf_tensor(name, shape, dt))

        def sem(name):
            return ctx.enter_context(nc.semaphore(name))

        def spread(ap, axis, n):
            new = ap.unsqueeze(axis)
            shape = list(new.shape)
            shape[axis] = n
            return new.broadcast_to(shape)

        def sems(name, n=L):
            return [sem(f"{name}{i}") for i in range(n)]

        x = sb("x", [P, NT, D])
        qkv = sb("qkv", [P, NT, 3 * D])
        q_parts = sb("q_parts", [P, NT, 3 * D], BF16)
        acc = sb("acc", [P, NT, MW])
        x_first = qkv[:, :, 0:D]
        kv = sb("kv", [P, SLOTS, GC, 2 * D])
        dst_hi = sb("dst_hi", [NG, GE], BF16)
        dst_lo = sb("dst_lo", [NG, GE], BF16)
        dst_col = sb("dst_col", [P, GC, NG])
        src_idx = sb("src_idx", [P, GC, NG], I32)
        idx = sb("idx", [P, SLOTS, GC], I32)
        pair_tab = sb("pair_tab", [1, NG + 2], I32)
        dist = sb("dist", [P, GE], BF16)
        hotT = sb("hotT", [P, 2, GE], BF16)
        hot = sb("hot", [P, 2, GC, P])
        prod = sb("prod", [P, GE])
        dots = sb("dots", [P, GC * H])
        not_nan = sb("not_nan", [P, GC * H])
        clipped = sb("clipped", [P, GC * H])
        att = sb("att", [P, GC * H])
        msg = sb("msg", [P, 2, GC, MW])
        pick = sb("pick", [NG, 2, P], BF16)
        ident = sb("ident", [P, P])
        ones = sb("ones", [P, P])
        zeros = sb("zeros", [P, 512], BF16)
        below = sb("below", [NG, NG])
        node_row = sb("node_row", [P, NT * P])
        neg_node = sb("neg_node", [P, NT])
        is_node = sb("is_node", [P, NT])
        eps_col = sb("eps_col", [P, 1])
        wfold = sb("wfold", [P, L, 3 * D])
        bfold = sb("bfold", [P, L, 3 * D])
        degw = sb("degw", [P, L, 3 * D])
        wo = sb("wo", [P, L, D])
        w1g = sb("w1g", [P, L, FF])
        b1f = sb("b1f", [P, L, FC])
        w2 = sb("w2", [P, L, FC, D])
        bo_bc = sb("bo_bc", [P, L, D])
        b2_bc = sb("b2_bc", [P, L, D])
        vecs = sb("vecs", [P, L, 7])
        cvec = sb("cvec", [P, 2])
        posT, pos1, c_bc, wd_bc = (hot[:, 0, k, :] for k in range(4))
        raw = hot[:, 1, :, :].rearrange("p c n -> p (c n)")
        wqkv, wpos, w1 = raw[:, 0:3 * D], raw[:, 3 * D:4 * D], raw[:, 4 * D:4 * D + FF]
        raw_rows = msg[:, 1, :, :].rearrange("p c n -> p (c n)")
        bqkv_row, b1_row = raw_rows[0:1, 0:3 * D], raw_rows[0:1, 3 * D:3 * D + FF]
        stats = sb("stats", [P, NT, 6])
        half_gap = sb("half_gap", [P, NT])
        mean2 = sb("mean2", [P, NT])
        sq_dev = sb("sq_dev", [P, NT])
        gap2 = sb("gap2", [P, NT])
        var = sb("var", [P, NT])
        sd = sb("sd", [P, NT])
        rstd = sb("rstd", [P, NT])
        nmr = sb("nmr", [P, NT])
        dev = sb("dev", [P, NT])
        dev2 = sb("dev2", [P, NT])
        degn = sb("degn", [P, NT])
        dcol = sb("dcol", [P, 4])
        rsum = sb("rsum", [P, NT, H])
        z = sb("z", [P, UN, D])
        zT = sb("zT", [P, UN, D])
        kv_flat = kv[:, :, :, :].rearrange("p s c d -> p (s c d)")

        def row_buf(k, dt=F32):
            return kv_flat[0:NG, k * GE:(k + 1) * GE].bitcast(dt) if dt != F32 else kv_flat[0:NG, k * GE:(k + 1) * GE]

        src_i, dst_i, src_f, dst_f, tmp_f = row_buf(0, I32), row_buf(1, I32), row_buf(2), row_buf(3), row_buf(4)
        tmp_i = row_buf(5, I32)
        tmp_j = row_buf(6, I32)
        ext = sb("ext", [NG, 2])
        ext_i = sb("ext_i", [NG, 2], I32)
        ext_t = sb("ext_t", [NG, 2], I32)
        tiles = sb("tiles", [NG, 2])
        npair = sb("npair", [NG, 1])
        pair_f = prod[0:1, 0:3 * (NG + 2)].rearrange("a (k g) -> a k g", g=NG + 2)
        qf = q_parts[:, :, :].rearrange("p t d -> p (t d)")
        ag = qf.bitcast(F32)[:, 0:NT * D].rearrange("p (t d) -> p t d", d=D)
        EC = NG * GC

        def carve(at, a, b):
            return qf[:, at:at + a * b].rearrange("p (a b) -> p a b", b=b)

        hot_lo = [carve(i * LO * HB, LO, HB) for i in range(2)]
        hot_hi = [carve(2 * LO * HB + i * HI * HB, HI, HB) for i in range(2)]
        AT = 2 * (LO + HI) * HB
        lo_ref = carve(AT, LO, HB)
        qkv_flat = qkv[:, :, :].rearrange("p t d -> p (t d)")
        hi_ref = qkv_flat[:, 0:HI * HB // 2].bitcast(BF16).rearrange("p (a b) -> p a b", b=HB)
        src_lo = qkv_flat[:, 1000:1000 + EC // 2].bitcast(BF16)
        src_hi = qkv_flat[:, 1400:1400 + EC // 2].bitcast(BF16)
        src_ci = qkv_flat[:, 2000:2000 + EC].bitcast(I32)
        lo_i = qkv_flat[:, 3000:3000 + EC].bitcast(I32)
        hi_i = qkv_flat[:, 4000:4000 + EC].bitcast(I32)
        self_dots, self_ok, self_clip, self_scores = (
            hot[:, 0, :, :].rearrange("p c n -> p (c n)")[:, k * NT * H:(k + 1) * NT * H] for k in range(4))
        hid = kv_flat[:, 0:UN * FF].rearrange("p (u f) -> p u f", u=UN)

        ps = ctx.enter_context(nc.psum_tensor("ps", [P, 8, 512], F32))
        qd = [ps[:, 2 * b:2 * b + 2, :].rearrange("p b n -> p (b n)") for b in range(2)]
        agg = ps[:, 4:6, 0:MW]
        dst_rows = ps[:, 6:8, :].rearrange("p b n -> p (b n)")
        tp = [ps[:, 5 + u % 3, 0:P] for u in range(UN)]
        wide = [ps[:, u, :] for u in range(UN)]
        cnt = ps[0:LO, 4, 0:HI]

        kv_tab = [nc.dram_tensor(f"kv_tab{l}", [NT * P, 2 * D], F32) for l in range(L)]

        rows_clear = sem("rows_clear")
        consts = sem("consts")
        edges_in = sem("edges_in")
        x_clear = sem("x_clear")
        x_in = sem("x_in")
        raw_in = sems("raw_in")
        kept_in = sems("kept_in")
        chain = sem("chain")
        src_rows = sem("src_rows")
        src_T = sem("src_T")
        dst_T = sem("dst_T")
        cols_read = sem("cols_read")
        hot_ready = sem("hot_ready")
        hot_used = sem("hot_used")
        dst_split = sem("dst_split")
        dst_parts = sem("dst_parts")
        ext_steps = sem("ext_steps")
        ext_ready = sem("ext_ready")
        npair_ready = sem("npair_ready")
        pair_ps = sem("pair_ps")
        tab_ready = sem("tab_ready")
        sq_ready = sem("sq_ready")
        sq_sum = sem("sq_sum")
        deg_sd = sem("deg_sd")
        f_pos = sem("f_pos")
        f_posT_ps = sem("f_posT_ps")
        f_posT = sem("f_posT")
        f_cols = sem("f_cols")
        f_w_ps = sem("f_w_ps")
        f_w = sem("f_w")
        f_b_ps = sem("f_b_ps")
        f_done = sem("f_done")
        act_chain = sem("act_chain")
        st_done = sems("st_done", 2 * L + 1)
        mv_done = sem("mv_done")
        sd_done = sem("sd_done")
        rstd_done = sem("rstd_done")
        nmr_done = sem("nmr_done")
        z_done = sems("z_done", 2 * L)
        tp_done = sems("tp_done", 2 * L)
        zT_done = sems("zT_done", 2 * L)
        qkv_ps = sems("qkv_ps")
        qkv_deg = sem("qkv_deg")
        qkv_done = sems("qkv_done")
        qkv_ahead = sem("qkv_ahead")
        tab_out = sems("tab_out")
        q_part = sems("q_part", 3)
        q_rest = sem("q_rest")
        self_prod = sem("self_prod")
        self_dot = sem("self_dot")
        self_mask = sem("self_mask")
        self_att = sem("self_att")
        self_exp = sem("self_exp")
        self_msg = sem("self_msg")
        idx_ready = sems("idx_ready")
        kv_in = [sems(f"kv_in{l}_", SLOTS) for l in range(L)]
        row_ready = sems("row_ready")
        dist_done = sems("dist_done")
        hotT_ready = sems("hotT_ready")
        hotT_used = sems("hotT_used")
        prod_done = sems("prod_done")
        dot_done = sems("dot_done")
        mask_done = sems("mask_done")
        att_done = sems("att_done")
        exp_done = sems("exp_done")
        msg_done = sems("msg_done")
        gathering = sems("gathering")
        hot_done = sems("hot_done")
        agg_done = sems("agg_done")
        evac_done = sems("evac_done")
        rs_done = sem("rs_done")
        bo_added = sems("bo_added")
        b2_added = sems("b2_added")
        picked = sems("picked")
        ag_done = sems("ag_done")
        agT_ps = sems("agT_ps")
        agT_done = sems("agT_done")
        o_ps = sems("o_ps")
        x2_done = sems("x2_done")
        h_ps = sems("h_ps")
        h_done = sems("h_done")
        y_ps = sems("y_ps")
        x3_done = sems("x3_done")
        first_in = sem("first_in")
        fin_add = sem("fin_add")
        fin_z = sem("fin_z")
        fin_z2 = sem("fin_z2")
        out_done = sem("out_done")

        block = ctx.enter_context(nc.Block())
        NCONST = 11
        RAW_LOADS = 16
        KEPT_LOADS = 4

        def pair_words(eng, base):
            read = {}

            def word(d):
                if d not in read:
                    w = eng.value_load(pair_tab[0:1, bass.ds(base + d + 2, 1)], min_val=0, max_val=MAXPAIRS * WORD + WORD - 1)
                    least = 0 if isinstance(base, int) and base + d < 0 else 1
                    read[d] = (eng.snap((w >> WORD_BITS).with_bounds(min_val=least, max_val=MAXPAIRS)),
                               eng.snap((w & (WORD - 1)).with_bounds(min_val=1, max_val=MAXPAIRS + TOFF)))
                return read[d]
            return word

        def tile_of(eng, pr, shift):
            return eng.snap((pr + TOFF - shift).with_bounds(min_val=0, max_val=NT - 1))

        def after(eng, semaphore, n):
            if not isinstance(n, int) or n > 0:
                eng.wait_ge(semaphore, n)

        def pipelined(eng, *stages):
            def step(s, v):
                for lag, stage in stages:
                    if not isinstance(s, int) or 0 <= s - lag < NT:
                        stage(s - lag, (v - lag) % UN)

            peeled = 1 + -(-max(lag for lag, _ in stages) // UN)
            for s in range(peeled * UN):
                step(s, s % UN)
            with eng.Fori(peeled, NU) as i:
                for v in range(UN):
                    step(UN * i + v, v)
            for s in range(NT, NT + max(lag for lag, _ in stages)):
                step(s, s % UN)

        def straight(eng, *stages):
            for s in range(NT + max(lag for lag, _ in stages)):
                for lag, stage in stages:
                    if 0 <= s - lag < NT:
                        stage(s - lag, (s - lag) % UN)

        def at(t):
            return bass.ds(t, 1)

        @block.sync
        def _(sp):
            sp.wait_ge(rows_clear, 2)
            for rows, d in ((src_i, src_d), (dst_i, dst_d)):
                sp.dma_start(rows[0:NG - 1, :], d[0:(NG - 1) * GE].rearrange("(g e) -> g e", e=GE)).then_inc(edges_in, 16)
                sp.dma_start(rows[NG - 1:NG, 0:ELAST], d[(NG - 1) * GE:E].rearrange("(g e) -> g e", g=1)).then_inc(edges_in, 16)
            sp.dma_start(x[:, 0:NT - 1, :], x_d[0:(NT - 1) * P, :].rearrange("(t p) d -> p t d", p=P)).then_inc(x_in, 16)
            sp.wait_ge(x_clear, 1)
            sp.dma_start(x[0:NLAST, NT - 1, :], x_d[(NT - 1) * P:N, :]).then_inc(x_in, 16)
            for l in range(L):
                after(sp, f_done, l)

                def load(to, what, done=raw_in):
                    sp.dma_start(to, what).then_inc(done[l], 16)
                load(wpos, W["Wpos"][l])
                for n, k in enumerate(("Wq", "Wk", "Wv")):
                    load(wqkv[:, n * D:(n + 1) * D], W[k][l])
                for n, k in enumerate(("ln1_g", "ln1_b", "ln2_g", "ln2_b", "bpos", "bdeg")):
                    load(vecs[:, l, n:n + 1], W[k][l:l + 1, :].rearrange("a p -> p a"))
                load(vecs[:, l, 6:7], W["Wdeg"][l].rearrange("a p -> p a"))
                for n, k in enumerate(("bq", "bk", "bv")):
                    load(bqkv_row[:, n * D:(n + 1) * D], W[k][l:l + 1, :])
                load(w1, W["W1"][l])
                load(b1_row, W["b1"][l:l + 1, :])
            for l in range(L):
                load(wo[:, l, :], W["Wo"][l], kept_in)
                load(w2[:, l, :, :], W["W2"][l].rearrange("(c p) n -> p c n", p=P), kept_in)
                load(bo_bc[:, l, :], W["bo"][l, :].partition_broadcast(P), kept_in)
                load(b2_bc[:, l, :], W["b2"][l, :].partition_broadcast(P), kept_in)
            for l in range(L):
                table = kv_tab[l][:, :].rearrange("(t p) d -> p t d", p=P)
                with sp.Fori(0, NU) as i:
                    sp.wait_ge(qkv_done[l], UN * i + UN)
                    sp.dma_start(table[:, bass.ds(UN * i, UN), :], qkv[:, bass.ds(UN * i, UN), D:3 * D]).then_inc(tab_out[l], 16)
            sp.wait_ge(self_msg, L * NU)
            sp.wait_ge(q_rest, L * NU)
            sp.wait_ge(tab_out[L - 1], 16 * NU)
            sp.dma_start(x_first[:, 0:NT - 1, :], x_d[0:(NT - 1) * P, :].rearrange("(t p) d -> p t d", p=P)).then_inc(first_in, 16)
            sp.dma_start(x_first[0:NLAST, NT - 1, :], x_d[(NT - 1) * P:N, :]).then_inc(first_in, 16)
            with sp.Fori(0, NU - 1) as i:
                sp.wait_ge(fin_z, i + 1)
                sp.wait_ge(fin_z2, i + 1)
                sp.dma_start(out_d[bass.ds(UN * P * i, UN * P), :].rearrange("(t p) d -> p t d", p=P),
                             x[:, bass.ds(UN * i, UN), :]).then_inc(out_done, 16)
            sp.wait_ge(fin_z, NU)
            sp.wait_ge(fin_z2, NU)
            sp.dma_start(out_d[(NT - UN) * P:(NT - 1) * P, :].rearrange("(t p) d -> p t d", p=P),
                         x[:, NT - UN:NT - 1, :]).then_inc(out_done, 16)
            sp.dma_start(out_d[(NT - 1) * P:N, :], x[0:NLAST, NT - 1, :]).then_inc(out_done, 16)
            sp.wait_ge(out_done, 16 * (NU + 1))

        @block.gpsimd
        def _(pool):
            pool.memset(src_i, -1).then_inc(rows_clear, 1)
            pool.memset(dst_i, -1).then_inc(rows_clear, 1)
            pool.memset(x[:, NT - 1, :], 0.0).then_inc(x_clear, 1)
            pool.memset(ident[:, :], 0.0).then_inc(consts, 1)
            pool.wait_ge(consts, 1)
            pool.affine_select(out=ident[:, :], in_=ident[:, :], compare_op=ALU.not_equal, fill=1.0, base=0,
                               pattern=[[-1, P]], channel_multiplier=1).then_inc(consts, 1)
            pool.iota(lo_ref, pattern=[[1, LO], [0, HB]], base=0, channel_multiplier=0,
                      allow_small_or_imprecise_dtypes=True).then_inc(consts, 1)
            pool.iota(hi_ref, pattern=[[1, HI], [0, HB]], base=0, channel_multiplier=0,
                      allow_small_or_imprecise_dtypes=True).then_inc(consts, 1)
            pool.memset(ones[:, :], 1.0).then_inc(consts, 1)
            pool.memset(is_node[:, :], 1.0).then_inc(consts, 1)
            pool.memset(zeros[:, :], 0.0).then_inc(consts, 1)
            pool.wait_ge(consts, 7)
            pool.affine_select(out=is_node[:, :], in_=is_node[:, :], compare_op=ALU.is_ge, fill=0.0, base=N - 1,
                               pattern=[[-P, NT]], channel_multiplier=-1).then_inc(consts, 1)
            pool.affine_select(out=below[:, :], in_=ones[0:NG, 0:NG], compare_op=ALU.is_ge, fill=0.0, base=-1,
                               pattern=[[1, NG]], channel_multiplier=-1).then_inc(consts, 1)
            pool.iota(neg_node[:, :], pattern=[[-P, NT]], base=0, channel_multiplier=-1,
                      allow_small_or_imprecise_dtypes=True).then_inc(consts, 1)
            pool.iota(node_row[:, :], pattern=[[1, NT * P]], base=0, channel_multiplier=0,
                      allow_small_or_imprecise_dtypes=True).then_inc(consts, 1)

            pool.wait_ge(src_rows, 2)
            nc.gpsimd.tensor_scalar(tmp_f, dst_f, 0.0, float(2 * NT * P), ALU.is_lt, ALU.mult).then_inc(ext_steps, 1)
            pool.wait_ge(ext_steps, 1)
            nc.gpsimd.tensor_tensor(tmp_f, tmp_f, dst_f, ALU.add).then_inc(ext_steps, 1)

            for l in range(L):
                pool.wait_ge(raw_in[l], 16 * RAW_LOADS)
                nc.gpsimd.tensor_tensor(pos1, wpos, ident[:, :], ALU.add).then_inc(f_pos, 1)

            for l in range(L):
                pool.wait_ge(kept_in[l], 16 * KEPT_LOADS)
                with pool.Fori(0, NT) as t:
                    pool.wait_ge(z_done[2 * l], t + 1)
                    nc.gpsimd.tensor_tensor(x[:, at(t), :], x[:, at(t), :], bo_bc[:, l, :].unsqueeze(1), ALU.add).then_inc(bo_added[l], 1)
                pool.wait_ge(tab_out[l], 16 * NU)

                def gather(u, i, g, first=False, chunks=GC):
                    pool.wait_ge(idx_ready[l], g + 1)
                    if not first:
                        pool.wait_ge(msg_done[l], g - SLOTS + 1)
                    pool.sem_inc(gathering[l], 1)
                    for c in range(chunks):
                        pool.indirect_dma_start(kv[:, u, c, :], None, kv_tab[l][:, :],
                                                bass.IndirectOffsetOnAxis(ap=idx[:, u, c:c + 1], axis=0)).then_inc(kv_in[l][u], 16)

                for u in range(SLOTS):
                    gather(u, 0, u, first=True)
                with pool.Fori(1, NG // SLOTS) as i:
                    for u in range(SLOTS):
                        gather(u, i, SLOTS * i + u)
                for u in range(NG % SLOTS):
                    gather(u, NG // SLOTS, NG // SLOTS * SLOTS + u, chunks=LAST_CHUNKS if u == NG % SLOTS - 1 else GC)
                with pool.Fori(0, NT) as t:
                    pool.wait_ge(z_done[2 * l + 1], t + 1)
                    nc.gpsimd.tensor_tensor(x[:, at(t), :], x[:, at(t), :], b2_bc[:, l, :].unsqueeze(1), ALU.add).then_inc(b2_added[l], 1)

        @block.scalar
        def _(act):
            links = [0]

            def link(ins):
                links[0] += 1
                ins.then_inc(act_chain, 1)
                act.wait_ge(act_chain, links[0])

            def stats_sd(k):
                act.wait_ge(mv_done, 3 * k + 3)
                nc.scalar.activation(sd[:, :], var[:, :], ACT.Sqrt, bias=eps_col[:, :]).then_inc(sd_done, 1)

            def normalise(k):
                def stage(t, u):
                    after(act, tp_done[k], t - UN + 1)
                    nc.scalar.activation(z[:, u:u + 1, :], x[:, at(t), :], ACT.Identity,
                                         bias=nmr[:, at(t)], scale=rstd[:, at(t)]).then_inc(z_done[k], 1)
                return stage

            act.wait_ge(dst_split, 1)
            nc.scalar.activation(dst_hi[:, :], tmp_i, ACT.Copy, scale=float(P)).then_inc(dst_parts, 1)
            nc.scalar.activation(dst_lo[:, :], tmp_j, ACT.Copy).then_inc(dst_parts, 1)
            stats_sd(0)
            for l in range(L):
                act.wait_ge(f_posT_ps, l + 1)
                nc.scalar.activation(posT, ps[:, 5, 0:P], ACT.Copy).then_inc(f_posT, 1)
                link(nc.scalar.activation(cvec[:, 0:1], ps[:, 5, P:P + 1], ACT.Identity, bias=vecs[:, l, 4:5]))
                link(nc.scalar.activation(cvec[:, 1:2], cvec[:, 0:1], ACT.Identity, bias=vecs[:, l, 5:6]))
                nc.scalar.activation(c_bc, ones[:, :], ACT.Copy, scale=cvec[:, 1:2])
                nc.scalar.activation(wd_bc, ones[:, :], ACT.Copy, scale=vecs[:, l, 6:7]).then_inc(f_cols, 1)
                act.wait_ge(f_w_ps, l + 1)
                nc.scalar.activation(wfold[:, l, :], ps[:, 6, 0:3 * D], ACT.Copy, scale=vecs[:, l, 0:1]).then_inc(f_w, 1)
                nc.scalar.activation(w1g[:, l, :], w1, ACT.Copy, scale=vecs[:, l, 2:3])
                act.wait_ge(f_b_ps, l + 1)
                nc.scalar.activation(bfold[:, l, :], ps[:, 7, 0:3 * D], ACT.Copy)
                nc.scalar.activation(degw[:, l, :], ps[:, 5, 0:3 * D], ACT.Copy)
                nc.scalar.activation(b1f[:, l, :], ps[:, 6, 0:FC], ACT.Copy).then_inc(f_done, 1)

            act.wait_ge(nmr_done, 1)
            for t in range(UN):
                normalise(0)(t, t)
            act.wait_ge(sq_sum, 1)
            nc.scalar.activation(dcol[:, 1:2], ps[:, 7, 0:1], ACT.Sqrt, scale=1.0 / (N - 1)).then_inc(deg_sd, 1)

            for l in range(L):
                if l:
                    stats_sd(2 * l)
                act.wait_ge(nmr_done, 2 * l + 1)

                def copy_zT(t, u):
                    act.wait_ge(tp_done[2 * l], t + 1)
                    after(act, qkv_ps[l], t - UN + 1)
                    nc.scalar.activation(zT[:, u, :], tp[u], ACT.Copy).then_inc(zT_done[2 * l], 1)
                def normalise_next(t, u):
                    if not (l == 0 and isinstance(t, int) and t < UN):
                        normalise(2 * l)(t, u)
                pipelined(act, (0, normalise_next), (1, copy_zT))
                def pick_rows(g):
                    nc.scalar.activation(pick[:, bass.ds(g % 2, 1), :], spread(ident[0:NG, at(g)], 2, P), ACT.Copy).then_inc(picked[l], 1)

                pick_rows(0)
                pick_rows(1)
                with act.Fori(0, NU) as i:
                    tb = bass.ds(UN * i, UN)
                    act.wait_ge(qkv_done[l], UN * i + UN)
                    nc.scalar.activation(q_parts[:, tb, 0:D], qkv[:, tb, 0:D], ACT.Copy).then_inc(q_part[0], 1)
                with act.Fori(0, NU) as i:
                    tb = bass.ds(UN * i, UN)
                    act.wait_ge(q_rest, l * NU + i + 1)
                    nc.scalar.activation(q_parts[:, tb, D:2 * D], acc[:, tb, 0:D], ACT.Copy).then_inc(q_part[1], 1)
                act.sem_inc(hotT_used[l], 2)
                act.sem_inc(hotT_ready[l], 1)
                if l == 0:
                    act.wait_ge(tab_ready, 1)

                def one_hots(word, d, g):
                    a = word(d - 1)[0]
                    b, shift = word(d)
                    act.wait_ge(row_ready[l], g + 1)
                    pick_rows(g + 2)
                    with act.Fori(a, b) as pr:
                        t = tile_of(act, pr, shift)
                        act.wait_ge(hotT_ready[l], pr + 1)
                        nc.scalar.activation(dist[:, :], dst_rows, ACT.Abs, bias=neg_node[:, at(t)]).then_inc(dist_done[l], 1)
                        act.wait_ge(dist_done[l], pr + 1)
                        act.wait_ge(hotT_used[l], pr + 1)
                        nc.scalar.activation(hotT[:, bass.ds(pr % 2, 1), :], dist[:, :], ACT.Relu, bias=1.0, scale=-1.0).then_inc(hotT_ready[l], 1)

                def weights(u, g):
                    act.wait_ge(att_done[l], g + 1)
                    nc.scalar.activation(msg[:, u % 2, :, D:MW], att[:, :].rearrange("p (c h) -> p c h", h=H), ACT.Exp,
                                         scale=1.0 / SCALE).then_inc(exp_done[l], 1)

                word = pair_words(act, 0)
                one_hots(word, 0, 0)
                act.wait_ge(self_att, l + 1)
                nc.scalar.activation(acc[:, :, D:MW], self_scores.rearrange("p (t h) -> p t h", h=H), ACT.Exp,
                                     scale=1.0 / SCALE).then_inc(self_exp, 1)
                one_hots(word, 1, 1)
                with act.Fori(0, NG // SLOTS) as i:
                    word = pair_words(act, SLOTS * i)
                    for u in range(SLOTS):
                        weights(u, SLOTS * i + u)
                        one_hots(word, u + 2, SLOTS * i + u + 2)
                weights(0, NG - 2)
                weights(1, NG - 1)
                def copy_agT(t, u):
                    act.wait_ge(agT_ps[l], t + 1)
                    after(act, o_ps[l], t - UN + 1)
                    nc.scalar.activation(zT[:, u, :], tp[u], ACT.Copy).then_inc(agT_done[l], 1)
                pipelined(act, (0, copy_agT))
                stats_sd(2 * l + 1)
                act.wait_ge(nmr_done, 2 * l + 1 + 1)

                def gelu(t, u):
                    act.wait_ge(h_ps[l], t + 1)
                    after(act, y_ps[l], t - UN + 1)
                    for c in range(FC):
                        last = nc.scalar.activation(hid[:, u, c * P:(c + 1) * P], wide[u][:, c * P:(c + 1) * P], ACT.Gelu,
                                                    bias=b1f[:, l, c:c + 1])
                    last.then_inc(h_done[l], 1)
                pipelined(act, (0, normalise(2 * l + 1)), (2, gelu))
            stats_sd(2 * L)
            act.wait_ge(nmr_done, 2 * L + 1)
            with act.Fori(0, NU) as i:
                for u in range(CLOSING_ACT):
                    t = at(UN * i + u)
                    last = nc.scalar.activation(x[:, t, :], x[:, t, :], ACT.Identity, bias=nmr[:, t], scale=rstd[:, t])
                last.then_inc(fin_z, 1)

        @block.vector
        def _(dve):
            links = [0]

            def link(ins):
                links[0] += 1
                ins.then_inc(chain, 1)
                dve.wait_ge(chain, links[0])

            def tile_stats(k, t):
                nc.vector.bn_stats(stats[:, at(t), :], x[:, at(t), :]).then_inc(st_done[k], 1)

            def variance(k):
                dve.wait_ge(st_done[k], NT)
                nc.vector.tensor_tensor(half_gap[:, :], stats[:, :, 1], stats[:, :, 4], ALU.subtract)
                nc.vector.tensor_tensor(mean2[:, :], stats[:, :, 1], stats[:, :, 4], ALU.add)
                nc.vector.tensor_tensor(sq_dev[:, :], stats[:, :, 2], stats[:, :, 5], ALU.add).then_inc(mv_done, 1)
                dve.wait_ge(mv_done, 3 * k + 1)
                nc.vector.scalar_tensor_tensor(out=gap2[:, :], in0=half_gap[:, :], scalar=0.25, in1=half_gap[:, :],
                                               op0=ALU.mult, op1=ALU.mult).then_inc(mv_done, 1)
                dve.wait_ge(mv_done, 3 * k + 2)
                nc.vector.scalar_tensor_tensor(out=var[:, :], in0=sq_dev[:, :], scalar=1.0 / D, in1=gap2[:, :],
                                               op0=ALU.mult, op1=ALU.add).then_inc(mv_done, 1)

            def scales(k):
                dve.wait_ge(sd_done, k + 1)
                nc.vector.reciprocal(rstd[:, :], sd[:, :]).then_inc(rstd_done, 1)
                dve.wait_ge(rstd_done, k + 1)
                nc.vector.scalar_tensor_tensor(out=nmr[:, :], in0=mean2[:, :], scalar=-0.5, in1=rstd[:, :],
                                               op0=ALU.mult, op1=ALU.mult).then_inc(nmr_done, 1)

            dve.sem_inc(self_dot, 1)
            link(nc.vector.memset(eps_col[:, :], EPS))
            link(nc.vector.memset(dev[:, :], 0.0))
            dve.wait_ge(edges_in, 64)
            nc.vector.tensor_copy(src_f, src_i).then_inc(src_rows, 1)
            nc.vector.tensor_copy(dst_f, dst_i).then_inc(src_rows, 1)
            nc.vector.tensor_single_scalar(tmp_i, dst_i, 7, ALU.arith_shift_right)
            nc.vector.tensor_single_scalar(tmp_j, dst_i, P - 1, ALU.bitwise_and).then_inc(dst_split, 1)
            dve.wait_ge(x_in, 32)
            for t in range(NT):
                tile_stats(0, t)
            variance(0)
            def cols(bank):
                return ps[:, bank:bank + 2, 0:4 * NG]
            dve.wait_ge(src_T, 1)
            link(nc.vector.tensor_copy(src_ci.rearrange("p (b n) -> p b n", b=2), cols(0)))
            link(nc.vector.tensor_single_scalar(lo_i, src_ci, LO - 1, ALU.bitwise_and))
            link(nc.vector.tensor_single_scalar(hi_i, src_ci, LO.bit_length() - 1, ALU.arith_shift_right))
            link(nc.vector.tensor_copy(src_lo, lo_i))
            link(nc.vector.tensor_copy(src_hi, hi_i))
            nc.vector.tensor_reduce(ext[:, 1:2], dst_f, AX.X, ALU.max)
            dve.wait_ge(ext_steps, 2)
            nc.vector.tensor_reduce(ext[:, 0:1], tmp_f, AX.X, ALU.min).then_inc(ext_ready, 1)
            dve.wait_ge(ext_ready, 1)
            link(nc.vector.tensor_copy(ext_i[:, :], ext[:, :]))
            link(nc.vector.tensor_single_scalar(ext_t[:, :], ext_i[:, :], 7, ALU.arith_shift_right))
            link(nc.vector.tensor_copy(tiles[:, :], ext_t[:, :]))
            nc.vector.scalar_tensor_tensor(out=npair[:, :], in0=tiles[:, 1:2], scalar=1.0, in1=tiles[:, 0:1],
                                           op0=ALU.add, op1=ALU.subtract).then_inc(npair_ready, 1)
            dve.wait_ge(dst_T, 1)
            nc.vector.tensor_copy(dst_col[:, :, :].rearrange("p (b c) g -> p b (c g)", b=2), cols(2)).then_inc(cols_read, 1)
            nc.vector.tensor_scalar(src_idx[:, :, :].rearrange("p (b c) g -> p b (c g)", b=2), cols(0), 0.0, None, ALU.max).then_inc(cols_read, 1)
            dve.wait_ge(pair_ps, 1)
            first_ps, count_ps, tile_ps = (ps[0:1, 7, 128 * k:128 * k + NG] for k in (1, 2, 3))
            link(nc.vector.memset(pair_f[:, 2, :], float(TOFF)))
            link(nc.vector.tensor_copy(pair_f[:, 0, 2:], first_ps))
            link(nc.vector.tensor_tensor(pair_f[:, 1, 2:], pair_f[:, 0, 2:], count_ps, ALU.add))
            link(nc.vector.scalar_tensor_tensor(out=pair_f[:, 0, 2:], in0=pair_f[:, 0, 2:], scalar=float(TOFF), in1=tile_ps,
                                                op0=ALU.add, op1=ALU.subtract))
            link(nc.vector.scalar_tensor_tensor(out=pair_f[:, 2, 2:], in0=pair_f[:, 1, 2:], scalar=float(WORD), in1=pair_f[:, 0, 2:],
                                                op0=ALU.mult, op1=ALU.add))
            nc.vector.tensor_copy(pair_tab[:, :], pair_f[:, 2, :]).then_inc(tab_ready, 1)
            scales(0)
            dve.wait_ge(consts, 4)
            with dve.Fori(0, NHB // 2) as i:
                for b in range(2):
                    k = 2 * i + b
                    dve.wait_ge(hot_used, k + 1)
                    nc.vector.tensor_tensor(hot_lo[b], lo_ref, spread(src_lo[:, bass.ds(k * HB, HB)], 1, LO), ALU.is_equal)
                    nc.vector.tensor_tensor(hot_hi[b], hi_ref, spread(src_hi[:, bass.ds(k * HB, HB)], 1, HI), ALU.is_equal).then_inc(hot_ready, 1)
            dve.wait_ge(hot_used, NHB + 2)
            dve.wait_ge(consts, NCONST)
            link(nc.vector.tensor_copy(dev[0:LO, 0:NT], cnt[:, 0:HI:2]))
            link(nc.vector.tensor_copy(dev[LO:2 * LO, 0:HI // 2], cnt[:, 1:HI:2]))
            link(nc.vector.scalar_tensor_tensor(out=dev[:, :], in0=dev[:, :], scalar=1.0 - MEAN_DEG, in1=is_node[:, :],
                                                op0=ALU.add, op1=ALU.mult))
            link(nc.vector.tensor_tensor(dev2[:, :], dev[:, :], dev[:, :], ALU.mult))
            nc.vector.tensor_reduce(dcol[:, 0:1], dev2[:, :], AX.X, ALU.add).then_inc(sq_ready, 1)
            dve.wait_ge(deg_sd, 1)
            link(nc.vector.tensor_scalar(dcol[:, 2:3], dcol[:, 1:2], 1e-6, None, ALU.add))
            link(nc.vector.reciprocal(dcol[:, 3:4], dcol[:, 2:3]))
            link(nc.vector.tensor_scalar(degn[:, :], dev[:, :], dcol[:, 3:4], None, ALU.mult))
            dve.wait_ge(tab_ready, 1)

            for l in range(L):
                if l == 0:
                    dve.wait_ge(f_done, L)
                    dve.wait_ge(tab_ready, 1)

                def fetch_idx(u, g):
                    nc.vector.tensor_copy(idx[:, u, :], src_idx[:, :, bass.ds(g, 1)].rearrange("p c o -> p (c o)")).then_inc(idx_ready[l], 1)
                if l == 0:
                    dve.wait_ge(cols_read, 2)
                for u in range(SLOTS):
                    fetch_idx(u, u)

                if l:
                    scales(2 * l)

                def add_products(t, u):
                    dve.wait_ge(qkv_ps[l], t + 1)
                    nc.vector.tensor_tensor(qkv[:, at(t), :], qkv[:, at(t), :], wide[u][:, 0:3 * D].unsqueeze(1), ALU.add).then_inc(qkv_done[l], 1)

                def degree_and_bias(t):
                    nc.vector.scalar_tensor_tensor(out=qkv[:, at(t), :], in0=degw[:, l + 1, :].unsqueeze(1), scalar=degn[:, at(t)],
                                                   in1=bfold[:, l + 1, :].unsqueeze(1), op0=ALU.mult, op1=ALU.add).then_inc(qkv_ahead, 1)

                def add_degree(t, u):
                    dve.wait_ge(qkv_ps[l], t + 1)
                    nc.vector.scalar_tensor_tensor(out=qkv[:, at(t), :], in0=degw[:, l, :].unsqueeze(1), scalar=degn[:, at(t)],
                                                   in1=wide[u][:, 0:3 * D].unsqueeze(1), op0=ALU.mult, op1=ALU.add).then_inc(qkv_deg, 1)

                def add_bias(t, u):
                    dve.wait_ge(qkv_deg, t + 1)
                    nc.vector.tensor_tensor(qkv[:, at(t), :], qkv[:, at(t), :], bfold[:, l, :].unsqueeze(1), ALU.add).then_inc(qkv_done[l], 1)
                if l == 0:
                    pipelined(dve, (0, add_degree), (1, add_bias))
                else:
                    dve.wait_ge(qkv_ahead, NT)
                    pipelined(dve, (0, add_products))

                def blocks():
                    return dve.Fori(0, NU)

                def rest(tb):
                    return acc[:, tb, 0:D]
                with blocks() as i:
                    tb = bass.ds(UN * i, UN)
                    dve.wait_ge(qkv_done[l], UN * i + UN)
                    dve.wait_ge(self_dot, l * NU + i + 1)
                    nc.vector.tensor_tensor(prod[:, 0:UN * D].rearrange("p (t d) -> p t d", d=D), qkv[:, tb, 0:D],
                                            qkv[:, tb, D:2 * D], ALU.mult).then_inc(self_prod, 1)
                    dve.wait_ge(q_part[0], l * NU + i + 1)
                    nc.vector.tensor_tensor(rest(tb), qkv[:, tb, 0:D], q_parts[:, tb, 0:D], ALU.subtract).then_inc(q_rest, 1)
                    dve.wait_ge(self_prod, l * NU + i + 1)
                    nc.vector.tensor_reduce(self_dots[:, bass.ds(UN * H * i, UN * H)],
                                            prod[:, 0:UN * D].rearrange("p (n d) -> p n d", d=HD), AX.X, ALU.add).then_inc(self_dot, 1)
                dve.wait_ge(self_dot, l * NU + NU + 1)
                nc.vector.tensor_tensor(self_ok, self_dots, self_dots, ALU.is_equal)
                nc.vector.tensor_scalar(self_clip, self_dots, CLIP * SCALE, -CLIP * SCALE, ALU.min, ALU.max).then_inc(self_mask, 1)
                dve.wait_ge(self_mask, l + 1)
                nc.vector.tensor_tensor(self_scores, self_clip, self_ok, ALU.mult).then_inc(self_att, 1)
                with blocks() as i:
                    tb = bass.ds(UN * i, UN)
                    dve.wait_ge(q_part[1], l * NU + i + 1)
                    nc.vector.tensor_tensor(q_parts[:, tb, 2 * D:3 * D], rest(tb), q_parts[:, tb, D:2 * D], ALU.subtract).then_inc(q_part[2], 1)
                dve.wait_ge(q_part[2], l * NU + NU)
                dve.wait_ge(self_exp, l + 1)
                with blocks() as i:
                    tb = bass.ds(UN * i, UN)
                    nc.vector.tensor_tensor(acc[:, tb, 0:D].rearrange("p t (h d) -> p t h d", d=HD),
                                            qkv[:, tb, 2 * D:3 * D].rearrange("p t (h d) -> p t h d", d=HD),
                                            spread(acc[:, tb, D:MW], 3, HD), ALU.mult).then_inc(self_msg, 1)
                dve.wait_ge(self_msg, l * NU + NU)

                dve.sem_inc(evac_done[l], 2)

                def evacuate(end, shift):
                    t = tile_of(dve, end - 1, shift)
                    dve.wait_ge(agg_done[l], end)
                    dve.wait_ge(evac_done[l], end + 1)
                    nc.vector.tensor_tensor(acc[:, at(t), :], acc[:, at(t), :],
                                            agg[:, bass.ds((end + 1) % 2, 1), :], ALU.add).then_inc(evac_done[l], 1)

                def one_hot(u, g, t):
                    nc.vector.tensor_tensor(hot[:, u % 2, :, :], spread(node_row[:, bass.ds(t * P, P)], 1, GC),
                                            dst_col[:, :, at(g)].broadcast_to([P, GC, P]), ALU.is_equal).then_inc(hot_done[l], 1)

                def further_tiles(u, g, a, b, shift):
                    with dve.If(b > a + 1):
                        with dve.Fori(a + 1, b) as pr:
                            dve.wait_ge(agg_done[l], pr)
                            one_hot(u, g, tile_of(dve, pr, shift))
                            evacuate(pr, shift)

                def edge_group(u, i, g, word, d, first=False, fetch=True, ahead=True):
                    half = msg[:, u % 2, :, :]
                    b, shift = word(d)
                    last_group = isinstance(g, int) and g == NG - 1
                    dve.wait_ge(kv_in[l][u], 16 * (GC * i + (LAST_CHUNKS if last_group else GC)))
                    dve.wait_ge(hotT_used[l], b + 2)
                    nc.vector.tensor_tensor(prod[:, :].rearrange("p (c d) -> p c d", d=D), kv[:, u, :, 0:D],
                                            qd[u % 2].rearrange("p (c d) -> p c d", d=D), ALU.mult).then_inc(prod_done[l], 1)
                    if fetch:
                        fetch_idx(u, g + SLOTS)
                    dve.wait_ge(prod_done[l], g + 1)
                    nc.vector.tensor_reduce(dots[:, :], prod[:, :].rearrange("p (n d) -> p n d", d=HD), AX.X, ALU.add).then_inc(dot_done[l], 1)
                    before_last, its_shift = word(d - 2)
                    if not first:
                        evacuate(before_last, its_shift)
                    dve.wait_ge(dot_done[l], g + 1)
                    nc.vector.tensor_tensor(not_nan[:, :], dots[:, :], dots[:, :], ALU.is_equal)
                    nc.vector.tensor_scalar(clipped[:, :], dots[:, :], CLIP * SCALE, -CLIP * SCALE, ALU.min, ALU.max).then_inc(mask_done[l], 1)
                    dve.wait_ge(mask_done[l], g + 1)
                    nc.vector.tensor_tensor(att[:, :], clipped[:, :], not_nan[:, :], ALU.mult).then_inc(att_done[l], 1)
                    a, last_shift = word(d - 1)
                    if not (isinstance(g, int) and g == 0):
                        further_tiles(u + 1, g - 1, before_last, a, last_shift)
                    one_hot(u, g, tile_of(dve, a, shift))
                    if ahead:
                        word(d + 1)
                    dve.wait_ge(exp_done[l], g + 1)
                    nc.vector.tensor_tensor(half[:, :, 0:D].rearrange("p c (h d) -> p c h d", d=HD),
                                            kv[:, u, :, D:2 * D].rearrange("p c (h d) -> p c h d", d=HD),
                                            spread(half[:, :, D:MW], 3, HD), ALU.mult).then_inc(msg_done[l], 1)

                word = pair_words(dve, 0)
                for g in range(SLOTS):
                    edge_group(g, 0, g, word, g, first=g < 2)
                with dve.Fori(1, NG // SLOTS - 1) as i:
                    word = pair_words(dve, SLOTS * i)
                    for u in range(SLOTS):
                        edge_group(u, i, SLOTS * i + u, word, u, ahead=u < SLOTS - 1)
                    if l < L - 1:
                        degree_and_bias(i - 1)
                word = pair_words(dve, 0)
                for g in range((NG // SLOTS - 1) * SLOTS, NG):
                    edge_group(g % SLOTS, g // SLOTS, g, word, g, fetch=g + SLOTS < NG, ahead=g < NG - 1)
                    if l < L - 1 and NG // SLOTS - 2 + g % SLOTS < NT and g < NG // SLOTS * SLOTS:
                        degree_and_bias(NG // SLOTS - 2 + g % SLOTS)
                end, shift = word(NG - 1)
                evacuate(*word(NG - 2))
                further_tiles(NG - 1, NG - 1, word(NG - 2)[0], end, shift)
                evacuate(end, shift)
                dve.wait_ge(evac_done[l], end + 2)

                nc.vector.reciprocal(rsum[:, :, :], acc[:, :, D:MW]).then_inc(rs_done, 1)
                dve.wait_ge(rs_done, l + 1)
                dve.wait_ge(bo_added[l], NT)

                def quotient(t, u):
                    if u == 0:
                        tb = bass.ds(t, UN)
                        nc.vector.tensor_tensor(ag[:, tb, :].rearrange("p t (h d) -> p t h d", d=HD),
                                                acc[:, tb, 0:D].rearrange("p t (h d) -> p t h d", d=HD),
                                                spread(rsum[:, tb, :], 3, HD), ALU.mult).then_inc(ag_done[l], UN)

                def residual(t, u):
                    if u in RESIDUAL_AT:
                        n = RESIDUAL_AT[u]
                        tb = bass.ds(t - n + 1, n)
                        dve.wait_ge(o_ps[l], t + 1)
                        nc.vector.tensor_tensor(x[:, tb, :], x[:, tb, :], ps[:, u - n + 1:u + 1, 0:D], ALU.add).then_inc(x2_done[l], n)
                        dve.wait_ge(x2_done[l], t + 1)
                        for k in range(n):
                            tile_stats(2 * l + 1, t - n + 1 + k)
                pipelined(dve, (0, quotient), (UN + 1, residual))
                variance(2 * l + 1)
                scales(2 * l + 1)

                def copy_zT(t, u):
                    dve.wait_ge(tp_done[2 * l + 1], t + 1)
                    after(dve, h_ps[l], t - UN + 1)
                    nc.vector.tensor_copy(zT[:, u, :], tp[u]).then_inc(zT_done[2 * l + 1], 1)

                def residual_2(t, u):
                    dve.wait_ge(b2_added[l], t + 1)
                    dve.wait_ge(y_ps[l], t + 1)
                    nc.vector.tensor_tensor(x[:, at(t), :], x[:, at(t), :], wide[u][:, 0:D].unsqueeze(1), ALU.add).then_inc(x3_done[l], 1)

                def residual_first(t, u):
                    dve.wait_ge(x3_done[l], t + 1)
                    nc.vector.tensor_tensor(x[:, at(t), :], x[:, at(t), :], x_first[:, at(t), :], ALU.add).then_inc(fin_add, 1)

                def stats_3(t, u):
                    if l == L - 1:
                        dve.wait_ge(fin_add, t + 1)
                    else:
                        dve.wait_ge(x3_done[l], t + 1)
                    tile_stats(2 * l + 2, t)
                if l == L - 1:
                    dve.wait_ge(first_in, 32)
                    pipelined(dve, (0, copy_zT), (3, residual_2), (4, residual_first), (5, stats_3))
                else:
                    pipelined(dve, (0, copy_zT), (3, residual_2), (4, stats_3))
                variance(2 * l + 2)
            scales(2 * L)
            dve.wait_ge(nmr_done, 2 * L + 1)
            with dve.Fori(0, NU) as i:
                for u in range(CLOSING_ACT, UN):
                    t = at(UN * i + u)
                    last = nc.vector.tensor_scalar(x[:, t, :], x[:, t, :], rstd[:, t], nmr[:, t], ALU.mult, ALU.add)
                last.then_inc(fin_z2, 1)

        @block.tensor
        def _(pe):
            MM = nc.tensor.matmul
            pe.sem_inc(hot_used, 2)
            pe.wait_ge(consts, 2)
            pe.wait_ge(src_rows, 2)
            for which, bank, done in ((src_f, 0, src_T), (dst_f, 2, dst_T)):
                for c in range(GC):
                    last = nc.tensor.transpose(ps[:, bank + c // 4, (c % 4) * NG:(c % 4 + 1) * NG], which[:, c * P:(c + 1) * P], ident[0:NG, 0:NG])
                last.then_inc(done, 1)
            def count(i):
                for b in range(2):
                    pe.wait_ge(hot_ready, 2 * i + b + 1)
                    for c in range(HB):
                        last = MM(cnt, hot_lo[b][:, :, c], hot_hi[b][:, :, c], start=False, stop=True, skip_group_check=True)
                    last.then_inc(hot_used, 1)

            pe.wait_ge(consts, NCONST)
            pe.wait_ge(npair_ready, 1)
            MM(ps[0:1, 7, 128:128 + NG], npair[:, :], below[:, :], start=True, stop=True)
            MM(ps[0:1, 7, 256:256 + NG], npair[:, :], ident[0:NG, 0:NG], start=True, stop=True)
            MM(ps[0:1, 7, 384:384 + NG], tiles[:, 0:1], ident[0:NG, 0:NG], start=True, stop=True).then_inc(pair_ps, 1)

            def fold_transpose(l):
                pe.wait_ge(f_pos, l + 1)
                after(pe, f_done, l)
                nc.tensor.transpose(ps[:, 5, 0:P], pos1, ident[:, :])
                MM(ps[:, 5, P:P + 1], pos1, vecs[:, l, 1:2], start=True, stop=True).then_inc(f_posT_ps, 1)

            def fold_weights(l):
                pe.wait_ge(f_posT, l + 1)
                MM(ps[:, 6, 0:3 * D], posT, wqkv, start=True, stop=True).then_inc(f_w_ps, 1)

            def fold_biases(l):
                pe.wait_ge(f_cols, l + 1)
                pe.wait_ge(tab_ready, 1)
                MM(ps[:, 7, 0:3 * D], c_bc, wqkv, start=True, stop=False)
                MM(ps[:, 7, 0:3 * D], ones[0:1, :], bqkv_row, start=False, stop=True)
                MM(ps[:, 5, 0:3 * D], wd_bc, wqkv, start=True, stop=True)
                pe.wait_ge(f_w, l + 1)
                for c in range(FC):
                    MM(ps[:, 6, c:c + 1], w1[:, c * P:(c + 1) * P], vecs[:, l, 3:4], start=True, stop=False)
                    last = MM(ps[:, 6, c:c + 1], b1_row[:, c * P:(c + 1) * P], ones[0:1, 0:1], start=False, stop=True)
                last.then_inc(f_b_ps, 1)

            pe.wait_ge(consts, 7)
            MM(cnt, zeros[:, 0:LO], zeros[:, 0:HI], start=True, stop=False, skip_group_check=True)
            for l in range(L):
                start = l * (FOLD_AT + 3)
                with pe.Fori(start, start + FOLD_AT) as i:
                    count(i)
                for k, fold in enumerate((fold_transpose, fold_weights, fold_biases)):
                    fold(l)
                    count(start + FOLD_AT + k)
            with pe.Fori(L * (FOLD_AT + 3), NHB // 2) as i:
                count(i)
            pe.wait_ge(sq_ready, 1)
            pe.wait_ge(f_done, L)
            MM(ps[:, 7, 0:1], ones[:, :], dcol[:, 0:1], start=True, stop=True).then_inc(sq_sum, 1)

            for l in range(L):
                def transposed(k):
                    def stage(t, u):
                        pe.wait_ge(z_done[k], t + 1)
                        after(pe, zT_done[k], t - 1)
                        nc.tensor.transpose(tp[u], z[:, u, :], ident[:, :]).then_inc(tp_done[k], 1)
                    return stage

                def project_qkv(t, u):
                    pe.wait_ge(zT_done[2 * l], t + 1)
                    after(pe, qkv_done[l] if l else qkv_deg, t - UN + 1)
                    MM(wide[u][:, 0:3 * D], zT[:, u, :], wfold[:, l, :], start=True, stop=True).then_inc(qkv_ps[l], 1)
                if l == 0:
                    pe.wait_ge(cols_read, 2)
                    pe.wait_ge(deg_sd, 1)
                pipelined(pe, (0, transposed(2 * l)), (1, project_qkv))

                if l == 0:
                    pe.wait_ge(dst_parts, 2)
                pe.wait_ge(qkv_done[l], NT)

                def broadcast_rows(gp, g, a):
                    pe.wait_ge(picked[l], g + 1)
                    if a is not None:
                        pe.wait_ge(dist_done[l], a)
                    for half in range(2):
                        cut = slice(512 * half, 512 * half + 512)
                        for part, start in ((dst_hi, True), (dst_lo, False)):
                            last = MM(dst_rows[:, cut], pick[:, gp, :], part[:, cut], start=start, stop=not start)
                    last.then_inc(row_ready[l], 1)

                def gather_q(u, g, a, b, shift):
                    if not (isinstance(g, int) and g < 2):
                        pe.wait_ge(prod_done[l], g - 1)
                    def gather_pair(pr, first):
                        t = tile_of(pe, pr, shift)
                        pe.wait_ge(hotT_ready[l], pr + 2)
                        for c in range(GC):
                            for k in range(3):
                                last = MM(qd[u % 2][:, c * P:(c + 1) * P], hotT[:, bass.ds(pr % 2, 1), c * P:(c + 1) * P],
                                          q_parts[:, at(t), k * D:(k + 1) * D], start=first and c % 4 == 0 and k == 0,
                                          stop=True, skip_group_check=True)
                        last.then_inc(hotT_used[l], 1)
                    gather_pair(a, True)
                    with pe.If(b > a + 1):
                        with pe.Fori(a + 1, b) as pr:
                            gather_pair(pr, False)

                def sum_pair(u, pr):
                    pe.wait_ge(hot_done[l], pr + 1)
                    pe.wait_ge(evac_done[l], pr + 1)
                    for c in range(GC):
                        last = MM(agg[:, bass.ds(pr % 2, 1), :], hot[:, u % 2, c, :], msg[:, u % 2, c, :], start=(c == 0), stop=(c == GC - 1))
                    last.then_inc(agg_done[l], 1)

                def sum_further(u, a, b):
                    with pe.If(b > a + 1):
                        with pe.Fori(a + 1, b) as pr:
                            sum_pair(u, pr)

                def pe_group(u, g, word, d, more=True, ahead=True):
                    if more:
                        gather_q(u + 1, g + 1, word(d)[0], *word(d + 1))
                    if ahead:
                        broadcast_rows(u % 2, g + 2, word(d + 1)[0])
                    if not (isinstance(g, int) and g == 0):
                        sum_further(u + 1, word(d - 2)[0], word(d - 1)[0])
                    pe.wait_ge(msg_done[l], g + 1)
                    sum_pair(u, word(d - 1)[0])

                word = pair_words(pe, 0)
                broadcast_rows(0, 0, None)
                pe.wait_ge(q_part[2], l * NU + NU)
                gather_q(0, 0, word(-1)[0], *word(0))
                broadcast_rows(1, 1, word(0)[0])
                for g in range(SLOTS):
                    pe_group(g, g, word, g)
                with pe.Fori(1, NG // SLOTS) as i:
                    word = pair_words(pe, SLOTS * i)
                    for u in range(SLOTS):
                        pe_group(u, SLOTS * i + u, word, u)
                word = pair_words(pe, 0)
                pe_group(0, NG - 2, word, NG - 2, ahead=False)
                pe_group(1, NG - 1, word, NG - 1, more=False, ahead=False)
                sum_further(1, word(NG - 2)[0], word(NG - 1)[0])

                def transpose_ag(t, u):
                    pe.wait_ge(ag_done[l], t + 1)
                    after(pe, agT_done[l], t - 1)
                    nc.tensor.transpose(tp[u], ag[:, t, :], ident[:, :]).then_inc(agT_ps[l], 1)

                def project_out(t, u):
                    pe.wait_ge(agT_done[l], t + 1)
                    after(pe, x2_done[l], t - UN + 1)
                    MM(wide[u][:, 0:D], zT[:, u, :], wo[:, l, :], start=True, stop=True).then_inc(o_ps[l], 1)
                straight(pe, (0, transpose_ag), (1, project_out))

                def hidden(t, u):
                    pe.wait_ge(zT_done[2 * l + 1], t + 1)
                    after(pe, x3_done[l], t - UN + 1)
                    for c in range(FC):
                        last = MM(wide[u][:, c * P:(c + 1) * P], w1g[:, l, c * P:(c + 1) * P], zT[:, u, :], start=True, stop=True)
                    last.then_inc(h_ps[l], 1)

                def project_ffn(t, u):
                    pe.wait_ge(h_done[l], t + 1)
                    for c in range(FC):
                        last = MM(wide[u][:, 0:D], hid[:, u, c * P:(c + 1) * P], w2[:, l, c, :], start=(c == 0), stop=(c == FC - 1))
                    last.then_inc(y_ps[l], 1)
                pipelined(pe, (0, transposed(2 * l + 1)), (1, hidden), (3, project_ffn))


_WEIGHTS = ["Wq", "bq", "Wk", "bk", "Wv", "bv", "Wo", "bo", "Wpos", "bpos", "Wdeg", "bdeg",
            "ln1_g", "ln1_b", "ln2_g", "ln2_b", "W1", "b1", "W2", "b2"]


def kernel(**inputs):
    import numpy as _np
    import concourse.bacc as _bacc
    from concourse import mybir as _mybir
    from concourse.bass_utils import run_bass_kernel_spmd as _run

    nc = _bacc.Bacc("TRN2", target_bir_lowering=False, num_devices=1)
    arrays = {}

    def given(name):
        a = _np.ascontiguousarray(inputs[name])
        arrays[f"in_{name}"] = a
        return nc.dram_tensor(f"in_{name}", a.shape, _mybir.dt.from_np(a.dtype), kind="ExternalInput").ap()

    x, src, dst = given("x"), given("src"), given("dst")
    weights = {k: given(f"L0_gnn_{k}") for k in _WEIGHTS}
    out = nc.dram_tensor("out_0", (N, D), _mybir.dt.float32, kind="ExternalOutput").ap()
    gnn_program(nc, x, src, dst, weights, out)
    r = _run(nc, [arrays], core_ids=[0])
    return r.results[0]["out_0"]
```
